# Optimizing a Trainium2 kernel written in Bass

```python
import numpy as np
import jax
import jax.numpy as jnp

def _softmax(x, axis=-1):
    return jax.nn.softmax(x, axis=axis)

def _gelu(x):
    return jax.nn.gelu(x, approximate=True)

def _silu(x):
    return jax.nn.silu(x)

def _sigmoid(x):
    return jax.nn.sigmoid(x)

def _layernorm(x, axis=-1, eps=1e-05):
    m = jnp.mean(x, axis=axis, keepdims=True)
    v = jnp.var(x, axis=axis, keepdims=True)
    return (x - m) / jnp.sqrt(v + eps)

def _scatter_add(tgt, idx, src, axis=0):
    return tgt.at[idx].add(src)

def _segment_sum(src, seg, n):
    return jax.ops.segment_sum(src, seg, n)
kernel_name = 'mk_hybrid_d1_jaxref_r8_b79f65'

def setup_inputs(seed: int=0):
    np.random.seed(seed)
    _w = jnp.asarray

    def _L0_attn_a_setup():
        import jax, jax.numpy as jnp
        import numpy as np
        HEADS = 16

        def _split_heads(t, h):
            b, y, hd = t.shape
            d = hd // h
            return t.reshape(b, y, h, d).transpose(0, 2, 1, 3).reshape(b * h, y, d)

        def _merge_heads(t, b, h):
            bh, y, d = t.shape
            return t.reshape(b, h, y, d).transpose(0, 2, 1, 3).reshape(b, y, h * d)
        key = jax.random.key(seed)
        ks = jax.random.split(key, 5)
        B, S, D = (8, 512, 128)
        scale = 1.0 / np.sqrt(D)
        x = jax.random.normal(ks[0], (B, S, D), dtype=jnp.float32)
        Wq = jax.random.normal(ks[1], (D, D), dtype=jnp.float32) * scale
        Wk = jax.random.normal(ks[2], (D, D), dtype=jnp.float32) * scale
        Wv = jax.random.normal(ks[3], (D, D), dtype=jnp.float32) * scale
        Wo = jax.random.normal(ks[4], (D, D), dtype=jnp.float32) * scale
        return {'x': x, 'Wq': Wq, 'Wk': Wk, 'Wv': Wv, 'Wo': Wo}
    _L0_attn_a_in = _L0_attn_a_setup()

    def _L0_attn_b_setup():
        import jax, jax.numpy as jnp
        import numpy as np
        B, T = (4, 256)
        D_MODEL = 128
        N_HEADS = 8
        HEAD_DIM = 32
        KV_LRANK = 64

        def _orthogonalize_per_head(w):
            chunks = w.reshape(N_HEADS, HEAD_DIM, D_MODEL)

            def ns(m):
                A = m @ m.T
                Bm = 1.5 * jnp.eye(HEAD_DIM, dtype=m.dtype) - 0.5 * A
                return Bm @ m
            return jax.vmap(ns)(chunks).reshape(w.shape)
        key = jax.random.key(seed)
        ks = jax.random.split(key, 6)

        def lin(k, out_dim, in_dim):
            bound = 1.0 / np.sqrt(in_dim)
            return jax.random.uniform(k, (out_dim, in_dim), jnp.float32, -bound, bound)
        Wq = _orthogonalize_per_head(lin(ks[0], N_HEADS * HEAD_DIM, D_MODEL))
        return {'x': jax.random.normal(ks[1], (B, T, D_MODEL), jnp.float32), 'Wq': Wq, 'Wkv_down': lin(ks[2], KV_LRANK, D_MODEL), 'Wk_up': lin(ks[3], N_HEADS * HEAD_DIM, KV_LRANK), 'Wv_up': lin(ks[4], N_HEADS * HEAD_DIM, KV_LRANK), 'Wo': lin(ks[5], D_MODEL, N_HEADS * HEAD_DIM)}
    _L0_attn_b_in = _L0_attn_b_setup()

    def _L0_ffn_setup():
        import jax, jax.numpy as jnp
        import numpy as np
        D_MODEL, D_FF, NUM_EXPERTS, RANK, TOP_K = (128, 512, 8, 16, 2)
        B, S = (8, 256)

        def _expert_ffn(h, wi_w, wo_w, A, Bm):
            inter = jnp.einsum('bsd,fd->bsf', h, wi_w)
            lora = jnp.einsum('bsr,fr->bsf', jnp.einsum('bsd,rd->bsr', h, A), Bm)
            inter = jax.nn.relu(inter + lora)
            return jnp.einsum('bsf,df->bsd', inter, wo_w)
        key = jax.random.key(seed)
        ks = jax.random.split(key, 8)
        hidden_states = jax.random.normal(ks[0], (B, S, D_MODEL), dtype=jnp.float32)
        wi_w = jax.random.normal(ks[1], (D_FF, D_MODEL), dtype=jnp.float32) * (1.0 / np.sqrt(D_MODEL))
        wo_w = jax.random.normal(ks[2], (D_MODEL, D_FF), dtype=jnp.float32) * (1.0 / np.sqrt(D_FF))
        lora_As = jax.random.uniform(ks[3], (NUM_EXPERTS, RANK, D_MODEL), dtype=jnp.float32, minval=-1.0, maxval=1.0) / np.sqrt(D_MODEL)
        lora_Bs = jax.random.normal(ks[4], (NUM_EXPERTS, D_FF, RANK), dtype=jnp.float32) * 0.02
        top_k_indices = jnp.arange(TOP_K, dtype=jnp.int32)
        top_k_values = jax.random.uniform(ks[5], (TOP_K,), dtype=jnp.float32)
        return {'hidden_states': hidden_states, 'wi_w': wi_w, 'wo_w': wo_w, 'lora_As': lora_As, 'lora_Bs': lora_Bs, 'top_k_indices': top_k_indices, 'top_k_values': top_k_values}
    _L0_ffn_in = _L0_ffn_setup()
    _d = {'L0_attn_a_x': _L0_attn_a_in['x'], 'L0_attn_a_Wq': _L0_attn_a_in['Wq'], 'L0_attn_a_Wk': _L0_attn_a_in['Wk'], 'L0_attn_a_Wv': _L0_attn_a_in['Wv'], 'L0_attn_a_Wo': _L0_attn_a_in['Wo'], 'L0_attn_b_Wq': _L0_attn_b_in['Wq'], 'L0_attn_b_Wkv_down': _L0_attn_b_in['Wkv_down'], 'L0_attn_b_Wk_up': _L0_attn_b_in['Wk_up'], 'L0_attn_b_Wv_up': _L0_attn_b_in['Wv_up'], 'L0_attn_b_Wo': _L0_attn_b_in['Wo'], 'L0_ffn_wi_w': _L0_ffn_in['wi_w'], 'L0_ffn_wo_w': _L0_ffn_in['wo_w'], 'L0_ffn_lora_As': _L0_ffn_in['lora_As'], 'L0_ffn_lora_Bs': _L0_ffn_in['lora_Bs'], 'L0_ffn_top_k_indices': _L0_ffn_in['top_k_indices'], 'L0_ffn_top_k_values': _L0_ffn_in['top_k_values']}
    _x0 = _d['L0_attn_a_x']
    _d['L0_attn_a_x'] = jax.random.normal(jax.random.fold_in(jax.random.key(seed), 1), (1, 2048, 128), dtype=_x0.dtype)
    del _x0
    return _d

def reference(L0_attn_a_x, L0_attn_a_Wq, L0_attn_a_Wk, L0_attn_a_Wv, L0_attn_a_Wo, L0_attn_b_Wq, L0_attn_b_Wkv_down, L0_attn_b_Wk_up, L0_attn_b_Wv_up, L0_attn_b_Wo, L0_ffn_wi_w, L0_ffn_wo_w, L0_ffn_lora_As, L0_ffn_lora_Bs, L0_ffn_top_k_indices, L0_ffn_top_k_values):

    def _L0_attn_a_ref(x, Wq, Wk, Wv, Wo):
        import jax, jax.numpy as jnp
        import numpy as np
        HEADS = 16

        def _split_heads(t, h):
            b, y, hd = t.shape
            d = hd // h
            return t.reshape(b, y, h, d).transpose(0, 2, 1, 3).reshape(b * h, y, d)

        def _merge_heads(t, b, h):
            bh, y, d = t.shape
            return t.reshape(b, h, y, d).transpose(0, 2, 1, 3).reshape(b, y, h * d)
        b = x.shape[0]
        h = HEADS
        q = _split_heads(x @ Wq.T, h)
        k = _split_heads(x @ Wk.T, h)
        v = _split_heads(x @ Wv.T, h)
        d = q.shape[-1]
        z = jnp.einsum('byq,byk->bkq', q, k) / jnp.sqrt(jnp.asarray(d, x.dtype))
        z = jax.nn.softmax(z, axis=-1)
        z = jnp.einsum('byz,bvy->bvz', z, v)
        z = _merge_heads(z, b, h)
        return z @ Wo.T

    def _L0_attn_b_ref(x, Wq, Wkv_down, Wk_up, Wv_up, Wo):
        import jax, jax.numpy as jnp
        import numpy as np
        B, T = (4, 256)
        D_MODEL = 128
        N_HEADS = 8
        HEAD_DIM = 32
        KV_LRANK = 64

        def _orthogonalize_per_head(w):
            chunks = w.reshape(N_HEADS, HEAD_DIM, D_MODEL)

            def ns(m):
                A = m @ m.T
                Bm = 1.5 * jnp.eye(HEAD_DIM, dtype=m.dtype) - 0.5 * A
                return Bm @ m
            return jax.vmap(ns)(chunks).reshape(w.shape)
        b, t, _ = x.shape
        q = (x @ Wq.T).reshape(b, t, N_HEADS, HEAD_DIM)
        kv_latent = x @ Wkv_down.T
        k = (kv_latent @ Wk_up.T).reshape(b, t, N_HEADS, HEAD_DIM)
        v = (kv_latent @ Wv_up.T).reshape(b, t, N_HEADS, HEAD_DIM)
        scale = HEAD_DIM ** (-0.5)
        scores = jnp.einsum('bqhd,bkhd->bhqk', q, k) * scale
        attn = jax.nn.softmax(scores, axis=-1)
        out = jnp.einsum('bhqk,bkhd->bqhd', attn, v)
        out = out.reshape(b, t, N_HEADS * HEAD_DIM)
        return out @ Wo.T

    def _L0_ffn_ref(hidden_states, wi_w, wo_w, lora_As, lora_Bs, top_k_indices, top_k_values):
        import jax, jax.numpy as jnp
        import numpy as np
        D_MODEL, D_FF, NUM_EXPERTS, RANK, TOP_K = (128, 512, 8, 16, 2)
        B, S = (8, 256)

        def _expert_ffn(h, wi_w, wo_w, A, Bm):
            inter = jnp.einsum('bsd,fd->bsf', h, wi_w)
            lora = jnp.einsum('bsr,fr->bsf', jnp.einsum('bsd,rd->bsr', h, A), Bm)
            inter = jax.nn.relu(inter + lora)
            return jnp.einsum('bsf,df->bsd', inter, wo_w)
        out = jnp.zeros_like(hidden_states)
        for k in range(top_k_values.shape[0]):
            A = jnp.take(lora_As, top_k_indices[k], axis=0)
            Bm = jnp.take(lora_Bs, top_k_indices[k], axis=0)
            out = out + top_k_values[k] * _expert_ffn(hidden_states, wi_w, wo_w, A, Bm)
        return out
    x = L0_attn_a_x
    x = x + _L0_attn_a_ref(_layernorm(x, axis=-1), L0_attn_a_Wq, L0_attn_a_Wk, L0_attn_a_Wv, L0_attn_a_Wo)
    x = x + _L0_ffn_ref(_layernorm(x, axis=-1), L0_ffn_wi_w, L0_ffn_wo_w, L0_ffn_lora_As, L0_ffn_lora_Bs, L0_ffn_top_k_indices, L0_ffn_top_k_values)
    x = x + _L0_attn_b_ref(_layernorm(x, axis=-1), L0_attn_b_Wq, L0_attn_b_Wkv_down, L0_attn_b_Wk_up, L0_attn_b_Wv_up, L0_attn_b_Wo)
    x = x + _L0_ffn_ref(_layernorm(x, axis=-1), L0_ffn_wi_w, L0_ffn_wo_w, L0_ffn_lora_As, L0_ffn_lora_Bs, L0_ffn_top_k_indices, L0_ffn_top_k_values)
    return x

_drawn_inputs = setup_inputs


def setup_inputs(seed=0):
    import zlib

    import numpy as np

    out = dict(_drawn_inputs(seed))
    spreads = {}
    factors = {'L0_attn_b_Wq': 27.593,
     'L0_attn_b_Wk_up': 27.705,
     'L0_ffn_top_k_values': 64.0,
     'L0_attn_b_Wkv_down': 3.29,
     'L0_attn_b_Wv_up': 3.08,
     'L0_attn_b_Wo': 3.076}
    for name, (base, spread) in spreads.items():
        noise = np.random.default_rng([zlib.crc32(name.encode()), seed]).standard_normal(out[name].shape)
        drawn = base * np.exp(spread * noise) if base else spread * noise
        out[name] = jnp.asarray(drawn.astype(out[name].dtype))
    for name, factor in factors.items():
        out[name] = (out[name] * factor).astype(out[name].dtype)
    return out
```

```python
import numpy as np
import concourse.bass as bass
from concourse import mybir
from contextlib import ExitStack



def build(nc, x_in, a_wqT, a_wkT, a_wv, a_woT, b_wqT, b_wdT, b_wkT, b_wvT, b_woT,
          wiT, woT, lora_a, lora_bT, top_idx, top_val, row_expert, out):
    f32, f16, i32 = mybir.dt.float32, mybir.dt.float16, mybir.dt.int32
    ALU, ACT, AX = mybir.AluOpType, mybir.ActivationFunctionType, mybir.AxisListType.X
    ds = bass.ds

    P = 128
    N, D = x_in.shape
    TT = N // P
    BK = 512
    TB = BK // P
    NB = TT // TB
    EPS = 1e-5
    A_HEADS = 16
    AD = D // A_HEADS
    H, HD, LR = 8, 32, b_wdT.shape[1]
    HG = 2
    SCALE = float(HD) ** -0.5
    QC = 256
    NCH = N // QC
    QT = QC // P
    KB = N // P
    KP = KB // 2
    SK = 3 * HD
    MROW = 16 * 2 * QT
    SR = SK + 2
    U = 8
    NM, NE = 2, 4
    F = wiT.shape[1]
    FT = F // P
    E2 = 2
    ER = lora_a.shape[0]

    ctx = ExitStack()
    with ctx:
        def sb(name, shape, dt=f32):
            return ctx.enter_context(nc.sbuf_tensor(name, shape, dt))

        def sem(name):
            return ctx.enter_context(nc.semaphore(name))

        x = sb("x", [P, TT, D])
        awq, awk, awv, awo = (sb(n, [P, D]) for n in ("awq", "awk", "awv", "awo"))
        bwq, bwd, bwk = sb("bwq", [P, H * HD]), sb("bwd", [P, LR]), sb("bwk", [LR, H * HD])
        bwv, bwo = sb("bwv", [LR, H * HD]), sb("bwo", [P, HG, D])
        wi, wo = sb("wi", [P, F]), sb("wo", [P, FT, D])
        la, lb = sb("la", [ER, D]), sb("lb", [ER, F])
        idx_i, rowx = sb("idx_i", [ER, E2], i32), sb("rowx", [ER, 1])
        tv = sb("tv", [P, E2])
        ident, zero16 = sb("ident", [P, P]), sb("zero16", [P, BK], f16)
        ones = sb("ones", [P, HD])
        idx_f, pick = sb("idx_f", [ER, E2]), sb("pick", [ER, E2])
        lbx = sb("lbx", [ER, E2, F])
        weff = sb("weff", [P, E2, F])
        stats, mean = sb("stats", [P, TT, 6]), sb("mean", [P, TT])
        std, rstd = sb("std", [P, TT]), sb("rstd", [P, TT])
        wide = sb("wide", [P, 2, N])
        h = wide[:, 0, :].rearrange("p (t d) -> p t d", d=D)
        hT = wide[:, 1, :]
        cmat, t1, zs = sb("cmat", [P, D]), sb("t1", [P, D]), sb("zs", [P, D])
        zmax, zsum, zrec = sb("zmax", [P, 1]), sb("zsum", [P, 1]), sb("zrec", [P, 1])
        ze, zn = sb("ze", [P, D]), sb("zn", [P, D])
        ntm, mix = sb("ntm", [P, D]), sb("mix", [P, D])
        r0, r1 = sb("r0", [P, 2, BK]), sb("r1", [P, 2, BK])
        r = sb("r", [P, FT, BK])
        latT = sb("latT", [LR, N])
        high, low = sb("high", [P, 2 * HG, N], f16), sb("low", [P, 2 * HG, N], f16)
        Qs, Ks = sb("Qs", [P, H, N], f16), sb("Ks", [P, H, N], f16)
        V = sb("V", [P, KB, H * HD])
        vst = sb("vst", [P, HG, 2, P])
        prob = high[:, :, :].bitcast(f32).rearrange("p s (h q) -> p (s h) q", q=QC).rearrange("p (k h) q -> p k h q", k=2)
        pair = low[:, 0:2, :].bitcast(f32).rearrange("p s (h q) -> p (s h) q", q=QC)
        mpart, mcol = sb("mpart", [P, H, U]), sb("mcol", [P, H * QT])
        mh, ml = sb("mh", [H * QT, P], f16), sb("ml", [H * QT, P], f16)
        oraw, osum = sb("oraw", [P, BK]), sb("osum", [P, BK])
        oT = wide

        ps = ctx.enter_context(nc.psum_tensor("ps", [P, 8, BK], f32))
        MB0, EB0, OB, SB = 0, NM, NM + NE, NM + NE + 1

        s_x, s_wa, s_wf, s_wb, s_out = (sem(n) for n in ("s_x", "s_wa", "s_wf", "s_wb", "s_out"))
        s_gp, s_dv, s_ac = sem("s_gp"), sem("s_dv"), sem("s_ac")
        s_const, s_pick, s_weffp, s_weff = sem("s_const"), sem("s_pick"), sem("s_weffp"), sem("s_weff")
        NLN = 4
        s_st, s_ve = sem("s_st"), sem("s_ve")
        s_std, s_h, s_tr, s_hT = sem("s_std"), sem("s_h"), sem("s_tr"), sem("s_hT")
        s_ap, s_az, s_am = sem("s_ap"), sem("s_az"), sem("s_am")
        s_ze, s_mask = sem("s_ze"), sem("s_mask")
        s_mixp, s_x1 = sem("s_mixp"), sem("s_x1")
        s_hid, s_r0, s_r1, s_r, s_y, s_xf = (sem(n) for n in ("s_hid", "s_r0", "s_r1", "s_r", "s_y", "s_xf"))
        s_lat, s_latc, s_qk, s_hi, s_lo, s_vp, s_vc = (sem(n) for n in ("s_lat", "s_latc", "s_qk", "s_hi", "s_lo", "s_vp", "s_vc"))
        s_stack, s_ones = sem("s_stack"), sem("s_ones")
        s_sm, s_maxed, s_mcol, s_mT, s_mneg, s_mrow = (sem(n) for n in ("s_sm", "s_maxed", "s_mcol", "s_mT", "s_mneg", "s_mrow"))
        s_se, s_p, s_pv, s_pair, s_sum, s_vst = (sem(n) for n in ("s_se", "s_p", "s_pv", "s_pair", "s_sum", "s_vst"))
        s_acc, s_evac, s_oT = sem("s_acc"), sem("s_evac"), sem("s_oT")
        s_wop, s_x3 = sem("s_wop"), sem("s_x3")

        block = ctx.enter_context(nc.Block())
        nat = lambda t: t.rearrange("(t p) d -> p t d", p=P)

        @block.sync
        def _(sp):
            for b in range(NB):
                sp.dma_start(x[:, b * TB:(b + 1) * TB, :], nat(x_in)[:, b * TB:(b + 1) * TB, :]).then_inc(s_x, 16)
            for dst, src in ((awk, a_wkT), (awq, a_wqT), (awv, a_wv), (awo, a_woT)):
                sp.dma_start(dst[:, :], src).then_inc(s_wa, 16)
            for dst, src in ((bwq, b_wqT), (bwd, b_wdT), (bwk, b_wkT), (bwv, b_wvT)):
                sp.dma_start(dst[:, :], src).then_inc(s_wb, 16)
            sp.dma_start(bwo[:, :, :], b_woT.rearrange("(g p) d -> p g d", p=P)).then_inc(s_wb, 16)

            for n, (stack, parts) in enumerate(((Ks, (high, low, high)), (Qs, (high, high, low)))):
                for g in range(HG):
                    slot = n * HG + g
                    sp.wait_ge(s_hi, NB * (slot + 1))
                    sp.wait_ge(s_lo, NB * (slot + 1))
                    for hh in range(H // HG):
                        for row, part in enumerate(parts):
                            sp.dma_start(stack[row * HD:(row + 1) * HD, g * 4 + hh, :],
                                         part[hh * HD:(hh + 1) * HD, slot, :]).then_inc(s_stack, 16)

            def max_rows(chunk):
                sp.wait_ge(s_mneg, 2 * chunk + 2)
                for row, part in ((SK, mh), (SK + 1, ml)):
                    for t in range(QT):
                        sp.dma_start(Qs[row:row + 1, :, ds(chunk * QC + t * P, P)],
                                     part[t * H:(t + 1) * H, :]).then_inc(s_mrow, 16)

            max_rows(0)
            with sp.Fori(0, NCH - 1) as c:
                max_rows(c + 1)
            for b in range(NB):
                sp.wait_ge(s_xf, NB + b + 2)
                sp.dma_start(nat(out)[:, b * TB:(b + 1) * TB, :], x[:, b * TB:(b + 1) * TB, :]).then_inc(s_out, 16)
            sp.wait_ge(s_out, 16 * NB)

        @block.gpsimd
        def _(gp):
            gp.memset(ident[:, :], 0.0).then_inc(s_gp, 1)
            gp.wait_ge(s_gp, 1)
            gp.affine_select(out=ident[:, :], in_=ident[:, :], compare_op=ALU.not_equal, fill=1.0,
                             base=0, pattern=[[-1, P]], channel_multiplier=1).then_inc(s_const, 1)
            gp.memset(ones[:, :], 1.0).then_inc(s_const, 1)
            gp.memset(zero16[:, :], 0.0).then_inc(s_const, 1)
            gp.wait_ge(s_const, 3)
            gp.memset(Ks[SK:SR, :, :], 1.0).then_inc(s_ones, 1)
            gp.wait_ge(s_ones, 1)
            gp.wait_ge(s_az, 3)
            blocks = zs[:, :].rearrange("p (b j) -> p b j", j=AD)
            gp.affine_select(out=blocks, in_=blocks, compare_op=ALU.is_ge, fill=-1e30, base=0,
                             pattern=[[-AD, A_HEADS], [0, AD]], channel_multiplier=1).then_inc(s_gp, 1)
            gp.wait_ge(s_gp, 2)
            gp.affine_select(out=blocks, in_=blocks, compare_op=ALU.is_ge, fill=-1e30, base=AD - 1,
                             pattern=[[AD, A_HEADS], [0, AD]], channel_multiplier=-1).then_inc(s_mask, 1)

            gp.wait_ge(s_vc, KB // 2)
            gp.sem_inc(s_pair, HG)
            G4 = 4
            with gp.Fori(0, NCH) as c:
                with gp.Fori(0, KP) as p:
                    n = c * KP + p
                    for g in range(HG):
                        gp.wait_ge(s_pv, n * 4 + (2 * g + 2))
                        gp.tensor_copy(vst[:, g, :, :], V[:, ds(p * 2, 2), g * P:(g + 1) * P]).then_inc(s_vst, 1)
                    for g in range(HG):
                        gp.wait_ge(s_p, n * U + (NE + 4 * g + 4))
                        gp.wait_ge(s_sum, n * HG + (g + 1))
                        hs = slice(g * G4, (g + 1) * G4)
                        gp.tensor_tensor(pair[:, hs, :], prob[:, 0, hs, :], prob[:, 1, hs, :],
                                         ALU.add).then_inc(s_pair, 1)

        @block.scalar
        def _(act):
            for dst, src in ((la, lora_a), (lb, lora_bT), (wi, wiT)):
                act.dma_start(dst[:, :], src).then_inc(s_wf, 16)
            act.dma_start(wo[:, :, :], woT.rearrange("(t p) d -> p t d", p=P)).then_inc(s_wf, 16)
            act.dma_start(rowx[:, :], row_expert).then_inc(s_wf, 16)
            act.dma_start(idx_i[:, :], top_idx.partition_broadcast(ER)).then_inc(s_wf, 16)
            act.dma_start(tv[:, :], top_val.partition_broadcast(P)).then_inc(s_wf, 16)

            def ln(k):
                act.wait_ge(s_ve, k + 1)
                act.activation(std[:, :], std[:, :], ACT.Sqrt).then_inc(s_std, 1)

            def transposed(k):
                for b in range(0, NB, 2):
                    act.wait_ge(s_tr, NB * k + b + 1)
                    act.copy(hT[:, b * BK:(b + 1) * BK], ps[:, b, :]).then_inc(s_hT, 1)

            def ffn(k):
                with act.Fori(0, NB) as c:
                    for ft in range(FT):
                        act.wait_ge(s_hid, c * FT + (k * NB * FT + ft + 1))
                        act.wait_ge(s_r, c * FT + (k * NB * FT + ft + 1))
                        act.activation(r0[:, ft % 2, :], ps[:, 2 * (ft % 2), :], ACT.Relu).then_inc(s_r0, 1)

            ln(0)
            transposed(0)
            act.wait_ge(s_am, 1)
            act.activation(ze[:, :], zs[:, :], ACT.Exp, bias=zmax[:, :], accum_out=zsum[:, :]).then_inc(s_ze, 1)
            ln(1)
            transposed(1)
            ffn(0)
            ln(2)
            transposed(2)
            for b in range(NB):
                act.wait_ge(s_lat, b + 1)
                act.copy(latT[:, b * BK:(b + 1) * BK], ps[0:LR, 4 + b, :]).then_inc(s_latc, 1)
            for n in range(2 * HG * NB):
                act.wait_ge(s_qk, n + 1)
                act.copy(high[:, n // NB, (n % NB) * BK:(n % NB + 1) * BK], ps[:, n % 4, :]).then_inc(s_hi, 1)
            for n in range(KB // 2):
                act.wait_ge(s_vp, n + 1)
                act.copy(V[:, 2 * n:2 * n + 2, :].rearrange("p a b -> p (a b)"), ps[:, 4 + n % 4, :]).then_inc(s_vc, 1)

            act.sem_inc(s_p, NE)
            with act.Fori(0, NCH) as c:
                with act.Fori(0, KP) as p:
                    n = c * KP + p
                    for u in range(U):
                        g, k, hp = u // 4, (u // 2) % 2, u % 2
                        if u % 4 == 0:
                            act.wait_ge(s_pair, n * HG + (g + 1))
                        if u % 2 == 0:
                            act.wait_ge(s_pv, n * 4 + (2 * g + k + 1))
                        act.wait_ge(s_se, n * U + (u + 1))
                        hs = slice(4 * g + 2 * hp, 4 * g + 2 * hp + 2)
                        act.activation(prob[:, k, hs, :].rearrange("p a b -> p (a b)"), ps[:, EB0 + u % NE, :],
                                       ACT.Exp, scale=SCALE).then_inc(s_p, 1)
                act.wait_ge(s_acc, c + 1)
                act.wait_ge(s_oT, c * HG + HG)
                act.copy(oraw[:, :], ps[:, OB, :]).then_inc(s_evac, 1)
            ln(3)
            transposed(3)
            ffn(1)

        @block.vector
        def _(dve):
            chain = [0]

            def link(ins):
                chain[0] += 1
                ins.then_inc(s_dv, 1)
                dve.wait_ge(s_dv, chain[0])

            def ln(k):
                UN = 4
                with dve.Fori(0, TT // UN) as q:
                    for j in range(UN):
                        dve.bn_stats(stats[:, ds(q * UN + j, 1), :], x[:, ds(q * UN + j, 1), :]).then_inc(s_st, 1)
                dve.wait_ge(s_st, TT * (k + 1))
                even, odd = stats[:, :, 1], stats[:, :, 4]
                link(dve.tensor_tensor(mean[:, :], even, odd, ALU.add))
                link(dve.tensor_tensor(std[:, :], even, odd, ALU.subtract))
                link(dve.tensor_tensor(std[:, :], std[:, :], std[:, :], ALU.mult))
                link(dve.scalar_tensor_tensor(std[:, :], std[:, :], D / 4.0, stats[:, :, 2], ALU.mult, ALU.add))
                link(dve.tensor_tensor(std[:, :], std[:, :], stats[:, :, 5], ALU.add))
                link(dve.tensor_scalar(mean[:, :], mean[:, :], 0.5, None, ALU.mult))
                dve.tensor_scalar(std[:, :], std[:, :], 1.0 / D, EPS, ALU.mult, ALU.add).then_inc(s_ve, 1)
                dve.wait_ge(s_std, k + 1)
                link(dve.reciprocal(rstd[:, :], std[:, :]))
                with dve.Fori(0, TT // UN) as q:
                    for j in range(UN):
                        t = ds(q * UN + j, 1)
                        dve.tensor_scalar(h[:, t, :], x[:, t, :], mean[:, t], rstd[:, t],
                                          ALU.subtract, ALU.mult).then_inc(s_h, 1)

            def transposed(k):
                for b in range(1, NB, 2):
                    dve.wait_ge(s_tr, NB * k + b + 1)
                    dve.tensor_copy(hT[:, b * BK:(b + 1) * BK], ps[:, b, :]).then_inc(s_hT, 1)

            def ffn(k):
                with dve.Fori(0, NB) as c:
                    for ft in range(FT):
                        n = c * FT + (k * NB * FT + ft)
                        dve.wait_ge(s_hid, n + 1)
                        dve.tensor_scalar(r1[:, ft % 2, :], ps[:, 2 * (ft % 2) + 1, :], 0.0, tv[:, 1:2],
                                          ALU.max, ALU.mult).then_inc(s_r1, 1)
                        dve.wait_ge(s_r1, n + 1)
                        dve.wait_ge(s_r0, n + 1)
                        dve.wait_ge(s_y, c + (k * NB + 1))
                        dve.scalar_tensor_tensor(r[:, ft, :], r0[:, ft % 2, :], tv[:, 0:1], r1[:, ft % 2, :],
                                                 ALU.mult, ALU.add).then_inc(s_r, 1)
                    dve.wait_ge(s_y, c + (k * NB + 2))
                    xs = x[:, ds(c * TB, TB), :].rearrange("p a b -> p (a b)")
                    dve.tensor_tensor(xs, ps[:, 4, :], xs, ALU.add).then_inc(s_xf, 1)

            dve.wait_ge(s_wf, 16 * 7)
            link(dve.tensor_copy(idx_f[:, :], idx_i[:, :]))
            link(dve.tensor_scalar(pick[:, :], idx_f[:, :], rowx[:, 0:1], None, ALU.is_equal))
            for e in range(E2):
                dve.tensor_scalar(lbx[:, e, :], lb[:, :], pick[:, e:e + 1], None, ALU.mult).then_inc(s_pick, 1)
            for e in range(E2):
                dve.wait_ge(s_weffp, e + 1)
                dve.tensor_tensor(weff[:, e, :], ps[:, 6 + e, :], wi[:, :], ALU.add).then_inc(s_weff, 1)
            dve.wait_ge(s_x, 16 * NB)
            ln(0)
            transposed(0)
            for n, dst in enumerate((cmat, t1)):
                dve.wait_ge(s_ap, n + 1)
                dve.tensor_copy(dst[:, :], ps[:, 4 + n, 0:D]).then_inc(s_az, 1)
            dve.wait_ge(s_ap, 3)
            dve.tensor_scalar(zs[:, :], ps[:, 6, 0:D], float(AD) ** -0.5, None, ALU.mult).then_inc(s_az, 1)
            dve.wait_ge(s_mask, 1)
            link(dve.reduce_max(zrec[:, :], zs[:, :], axis=AX))
            dve.tensor_scalar(zmax[:, :], zrec[:, :], -1.0, None, ALU.mult).then_inc(s_am, 1)
            dve.wait_ge(s_ze, 1)
            dve.wait_ge(s_am, 1)
            link(dve.reciprocal(zrec[:, :], zsum[:, :]))
            dve.tensor_scalar(zn[:, :], ze[:, :], zrec[:, 0:1], None, ALU.mult).then_inc(s_az, 1)
            for n, dst in enumerate((ntm, mix)):
                dve.wait_ge(s_ap, n + 4)
                dve.tensor_copy(dst[:, :], ps[:, 4 + n, 0:D]).then_inc(s_az, 1)
            for b in range(NB):
                dve.wait_ge(s_mixp, b + 1)
                xs = x[:, b * TB:(b + 1) * TB, :].rearrange("p a b -> p (a b)")
                dve.tensor_tensor(xs, ps[:, b, :], xs, ALU.add).then_inc(s_x1, 1)
            dve.wait_ge(s_x1, NB)
            dve.sem_inc(s_r, 2)
            ln(1)
            transposed(1)
            ffn(0)
            dve.wait_ge(s_xf, NB + 1)
            ln(2)
            transposed(2)
            for n in range(2 * HG * NB):
                cols = slice((n % NB) * BK, (n % NB + 1) * BK)
                dve.wait_ge(s_hi, n + 1)
                dve.tensor_tensor(low[:, n // NB, cols], ps[:, n % 4, :], high[:, n // NB, cols],
                                  ALU.subtract).then_inc(s_lo, 1)

            dve.sem_inc(s_maxed, NM)
            dve.sem_inc(s_oT, HG)

            def maxima(chunk):
                with dve.Fori(0, H) as hd:
                    for u in range(U):
                        dve.wait_ge(s_sm, chunk * H * U + (hd * U + (u + 1)))
                        dve.reduce_max(mpart[:, ds(hd, 1), u:u + 1], ps[:, MB0 + u % NM, :], axis=AX).then_inc(s_maxed, 1)
                dve.wait_ge(s_maxed, chunk * H * U + (H * U + NM))
                dve.reduce_max(mcol[:, :].rearrange("p (t h) -> p t h", t=QT),
                               mpart[:, :, :].rearrange("p h (t j) -> p t h j", t=QT),
                               axis=AX).then_inc(s_mcol, 1)
                dve.wait_ge(s_mT, chunk + 1)
                dve.wait_ge(s_mrow, chunk * MROW)
                mT = ps[0:H * QT, MB0, 0:P]
                dve.tensor_scalar(mh[:, :], mT, -1.0, None, ALU.mult).then_inc(s_mneg, 1)
                dve.wait_ge(s_mneg, chunk * 2 + 1)
                dve.scalar_tensor_tensor(ml[:, :], mT, -1.0, mh[:, :], ALU.mult, ALU.subtract).then_inc(s_mneg, 1)

            def evacuate(chunk):
                dve.wait_ge(s_acc, chunk + 1)
                dve.wait_ge(s_oT, chunk * HG + HG)
                dve.reciprocal(osum[:, :], ps[:, SB, :]).then_inc(s_evac, 1)
                dve.wait_ge(s_evac, chunk * 2 + 4)
                for g in range(HG):
                    dve.tensor_tensor(oT[:, g, ds(chunk * QC, QC)], oraw[:, g * QC:(g + 1) * QC],
                                      osum[:, g * QC:(g + 1) * QC], ALU.mult).then_inc(s_oT, 1)

            maxima(0)
            with dve.Fori(0, NCH - 1) as c:
                maxima(c + 1)
                evacuate(c)
            evacuate(NCH - 1)
            for b in range(NB):
                dve.wait_ge(s_wop, b + 1)
                xs = x[:, b * TB:(b + 1) * TB, :].rearrange("p a b -> p (a b)")
                dve.tensor_tensor(xs, ps[:, b, :], xs, ALU.add).then_inc(s_x3, 1)
            dve.wait_ge(s_x3, NB)
            ln(3)
            transposed(3)
            ffn(1)

        @block.tensor
        def _(pe):
            mm = pe.matmul

            def transposed(k):
                for b in range(NB):
                    pe.wait_ge(s_h, TT * k + (b + 1) * TB)
                    for t in range(TB):
                        last = pe.transpose(ps[:, b, t * P:(t + 1) * P], h[:, b * TB + t, :], ident[:, :])
                    last.then_inc(s_tr, 1)

            def ffn(k):
                pe.wait_ge(s_hT, NB * (k * 2 + 2))
                with pe.Fori(0, NB) as c:
                    for ft in range(FT):
                        pe.wait_ge(s_r, c * FT + (k * NB * FT + ft + 1))
                        for e in range(E2):
                            last = mm(ps[:, 2 * (ft % 2) + e, :], weff[:, e, ft * P:(ft + 1) * P],
                                      hT[:, ds(c * BK, BK)], start=True, stop=True)
                        last.then_inc(s_hid, 1)
                    pe.wait_ge(s_r, c * FT + (k * NB * FT + FT + 2))
                    pe.wait_ge(s_xf, c + (k * NB + 1))
                    for t in range(TB):
                        for ft in range(FT):
                            last = mm(ps[:, 4, t * P:(t + 1) * P], r[:, ft, t * P:(t + 1) * P], wo[:, ft, :],
                                      start=(ft == 0), stop=(ft == FT - 1))
                    last.then_inc(s_y, 1)

            pe.wait_ge(s_const, 3)
            for e in range(E2):
                pe.wait_ge(s_pick, e + 1)
                mm(ps[:, 6 + e, :], la[:, :], lbx[:, e, :], start=True, stop=True).then_inc(s_weffp, 1)
            transposed(0)
            pe.wait_ge(s_wa, 64)
            for t in range(TT):
                last = mm(ps[:, 4, 0:D], h[:, t, :], h[:, t, :], start=(t == 0), stop=(t == TT - 1))
            last.then_inc(s_ap, 1)
            pe.wait_ge(s_az, 1)
            mm(ps[:, 5, 0:D], cmat[:, :], awk[:, :], start=True, stop=True).then_inc(s_ap, 1)
            pe.wait_ge(s_az, 2)
            pe.wait_ge(s_weff, E2)
            mm(ps[:, 6, 0:D], t1[:, :], awq[:, :], start=True, stop=True).then_inc(s_ap, 1)
            pe.wait_ge(s_az, 4)
            mm(ps[:, 4, 0:D], zn[:, :], awv[:, :], start=True, stop=True).then_inc(s_ap, 1)
            pe.wait_ge(s_az, 5)
            mm(ps[:, 5, 0:D], ntm[:, :], awo[:, :], start=True, stop=True).then_inc(s_ap, 1)
            pe.wait_ge(s_az, 6)
            pe.wait_ge(s_hT, NB)
            for b in range(NB):
                for t in range(b * TB, (b + 1) * TB):
                    last = mm(ps[:, b, (t % TB) * P:(t % TB + 1) * P], hT[:, t * P:(t + 1) * P], mix[:, :],
                              start=True, stop=True)
                last.then_inc(s_mixp, 1)
            pe.wait_ge(s_x1, NB)
            pe.sem_inc(s_y, 1)
            pe.sem_inc(s_xf, 1)
            transposed(1)
            ffn(0)
            pe.wait_ge(s_xf, NB + 1)
            transposed(2)
            pe.wait_ge(s_hT, 3 * NB)
            pe.wait_ge(s_wb, 16 * 5)
            for b in range(NB):
                mm(ps[0:LR, 4 + b, :], bwd[:, :], hT[:, b * BK:(b + 1) * BK], start=True, stop=True).then_inc(s_lat, 1)
            pe.wait_ge(s_latc, NB)
            for n in range(2 * HG * NB):
                g, b = (n // NB) % HG, n % NB
                w, rhs = (bwk, latT) if n < HG * NB else (bwq, hT)
                if n >= 4:
                    pe.wait_ge(s_lo, n - 3)
                mm(ps[:, n % 4, :], w[:, g * P:(g + 1) * P], rhs[:, b * BK:(b + 1) * BK],
                   start=True, stop=True).then_inc(s_qk, 1)
            for n in range(KB // 2):
                if n >= 4:
                    pe.wait_ge(s_vc, n - 3)
                for k in range(2):
                    kb = 2 * n + k
                    last = mm(ps[:, 4 + n % 4, k * H * HD:(k + 1) * H * HD], latT[:, kb * P:(kb + 1) * P], bwv[:, :],
                              start=True, stop=True)
                last.then_inc(s_vp, 1)
            pe.wait_ge(s_vc, KB // 2)
            pe.wait_ge(s_lo, 2 * HG * NB)
            pe.wait_ge(s_ones, 1)
            pe.wait_ge(s_stack, 16 * 2 * H * 3)
            pe.sem_inc(s_pv, 4)
            pe.sem_inc(s_sum, HG)
            pe.sem_inc(s_evac, 0 + 2)

            def score_max(chunk, hd, u):
                t, j = u // 4, u % 4
                pe.wait_ge(s_maxed, chunk * H * U + (hd * U + (u + 1)))
                mm(ps[:, MB0 + u % NM, :], Qs[0:SK, ds(hd, 1), ds(chunk * QC + t * P, P)],
                   Ks[0:SK, ds(hd, 1), j * BK:(j + 1) * BK], start=True, stop=True).then_inc(s_sm, 1)

            def max_transpose(chunk):
                pe.wait_ge(s_mcol, chunk + 1)
                pe.transpose(ps[0:H * QT, MB0, 0:P], mcol[:, :], ident[:, :]).then_inc(s_mT, 1)

            def score_exp(chunk, p, u):
                g, k, hp = u // 4, (u // 2) % 2, u % 2
                pe.wait_ge(s_p, (chunk * KP + p) * U + (u + 1))
                for a in range(2):
                    hd = 4 * g + 2 * hp + a
                    last = mm(ps[:, EB0 + u % NE, a * QC:(a + 1) * QC], Ks[0:SR, hd, ds(p * 2 * P + k * P, P)],
                              Qs[0:SR, hd, ds(chunk * QC, QC)], start=True, stop=True)
                last.then_inc(s_se, 1)

            def weigh(n, g, k):
                if k == 0:
                    pe.wait_ge(s_vst, n * HG + (g + 1))
                pe.wait_ge(s_p, n * U + (NE + 4 * g + 2 * k + 2))
                for j in range(4):
                    last = mm(ps[j * HD:(j + 1) * HD, OB, g * QC:(g + 1) * QC], vst[:, g, k, j * HD:(j + 1) * HD],
                              prob[:, k, 4 * g + j, :], start=False, stop=True, skip_group_check=True)
                last.then_inc(s_pv, 1)

            def total(n, g):
                pe.wait_ge(s_pair, n * HG + (HG + g + 1))
                for j in range(4):
                    last = mm(ps[j * HD:(j + 1) * HD, SB, g * QC:(g + 1) * QC], ones[:, :], pair[:, 4 * g + j, :],
                              start=False, stop=True, skip_group_check=True)
                last.then_inc(s_sum, 1)

            def attend(c, with_max):
                pe.wait_ge(s_evac, c * 2 + 2)
                for bank in (OB, SB):
                    mm(ps[:, bank, :], zero16[:, 0:P], zero16[:, :], start=True, stop=True)
                pe.wait_ge(s_mrow, c * MROW + MROW)

                def iteration(p, first):
                    n = c * KP + p
                    for u in range(U):
                        if with_max:
                            score_max(c + 1, p, u)
                        score_exp(c, p, u)
                        if u == 1 and not first:
                            weigh(n - 1, 1, 1)
                        if u == 2 and not first:
                            total(n - 1, 0)
                        if u == 3:
                            weigh(n, 0, 0)
                        if u == 5:
                            weigh(n, 0, 1)
                        if u == 6 and not first:
                            total(n - 1, 1)
                        if u == 7:
                            weigh(n, 1, 0)

                iteration(0, True)
                with pe.Fori(1, KP) as p:
                    iteration(p, False)
                n = c * KP + (KP - 1)
                weigh(n, 1, 1)
                total(n, 0)
                pe.wait_ge(s_pair, n * HG + (HG + 2))
                for j in range(4):
                    last = mm(ps[j * HD:(j + 1) * HD, SB, QC:2 * QC], ones[:, :], pair[:, 4 + j, :],
                              start=False, stop=True, skip_group_check=True)
                last.then_inc(s_sum, 1)

            def finish_chunk():
                mm(ps[:, SB, 0:2], zero16[:, 0:P], zero16[:, 0:2], start=False, stop=True,
                   skip_group_check=True).then_inc(s_acc, 1)

            with pe.Fori(0, H) as hd:
                for u in range(U):
                    score_max(0, hd, u)
            max_transpose(0)
            with pe.Fori(0, NCH - 1) as c:
                attend(c, True)
                finish_chunk()
                max_transpose(c + 1)
            attend(NCH - 1, False)
            finish_chunk()

            pe.wait_ge(s_oT, HG * (NCH + 1))
            for b in range(NB):
                for t in range(b * TB, (b + 1) * TB):
                    for g in range(HG):
                        last = mm(ps[:, b, (t % TB) * P:(t % TB + 1) * P], oT[:, g, t * P:(t + 1) * P], bwo[:, g, :],
                                  start=(g == 0), stop=(g == HG - 1))
                last.then_inc(s_wop, 1)
            pe.wait_ge(s_x3, NB)
            transposed(3)
            ffn(1)


def kernel(**inputs):
    import concourse.bacc as bacc
    from concourse.bass_utils import run_bass_kernel_spmd

    a = {k: np.asarray(v) for k, v in inputs.items()}
    T = lambda v: np.ascontiguousarray(v.T)
    x = a["L0_attn_a_x"]
    experts, rank, d = a["L0_ffn_lora_As"].shape
    f = a["L0_ffn_lora_Bs"].shape[1]
    arrays = {
        "x_in": np.ascontiguousarray(x.reshape(-1, d)),
        "a_wqT": T(a["L0_attn_a_Wq"]), "a_wkT": T(a["L0_attn_a_Wk"]),
        "a_wv": np.ascontiguousarray(a["L0_attn_a_Wv"]), "a_woT": T(a["L0_attn_a_Wo"]),
        "b_wqT": T(a["L0_attn_b_Wq"]), "b_wdT": T(a["L0_attn_b_Wkv_down"]),
        "b_wkT": T(a["L0_attn_b_Wk_up"]), "b_wvT": T(a["L0_attn_b_Wv_up"]), "b_woT": T(a["L0_attn_b_Wo"]),
        "wiT": T(a["L0_ffn_wi_w"]), "woT": T(a["L0_ffn_wo_w"]),
        "lora_a": np.ascontiguousarray(a["L0_ffn_lora_As"].reshape(experts * rank, d)),
        "lora_bT": np.ascontiguousarray(a["L0_ffn_lora_Bs"].transpose(0, 2, 1).reshape(experts * rank, f)),
        "top_idx": np.ascontiguousarray(a["L0_ffn_top_k_indices"]),
        "top_val": np.ascontiguousarray(a["L0_ffn_top_k_values"]),
        "row_expert": np.repeat(np.arange(experts, dtype=np.float32), rank)[:, None],
    }
    nc = bacc.Bacc("TRN2", target_bir_lowering=False, num_devices=1)
    aps = [nc.dram_tensor(k, v.shape, mybir.dt.from_np(v.dtype), kind="ExternalInput").ap() for k, v in arrays.items()]
    out = nc.dram_tensor("out", arrays["x_in"].shape, mybir.dt.float32, kind="ExternalOutput").ap()
    build(nc, *aps, out)
    r = run_bass_kernel_spmd(nc, [arrays], core_ids=[0])
    return r.results[0]["out"].reshape(x.shape)
```

```python
import numpy as np
import concourse.bass as bass
from concourse import mybir
from contextlib import ExitStack



def build(nc, x_in, a_wqT, a_wkT, a_wv, a_woT, b_wqT, b_wdT, b_wkT, b_wvT, b_woT,
          wiT, woT, lora_a, lora_bT, top_idx, top_val, row_expert, out):
    f32, f16, i32 = mybir.dt.float32, mybir.dt.float16, mybir.dt.int32
    ALU, ACT, AX = mybir.AluOpType, mybir.ActivationFunctionType, mybir.AxisListType.X
    ds = bass.ds

    P = 128
    N, D = x_in.shape
    TT = N // P
    BK = 512
    TB = BK // P
    NB = TT // TB
    EPS = 1e-5
    A_HEADS = 16
    AD = D // A_HEADS
    H, HD, LR = 8, 32, b_wdT.shape[1]
    HPG = 4
    HG = 2
    SCALE = float(HD) ** -0.5
    QC = 256
    NCH = N // QC
    QT = QC // P
    KB = N // P
    KP = KB // 2
    SK = 3 * HD
    MROW = 16 * 2
    SR = SK + 2
    U = 8
    SUM_SLOT = 5
    NM, NE = 4, 2
    F = wiT.shape[1]
    FT = F // P
    E2 = 2
    ER = lora_a.shape[0]

    ctx = ExitStack()
    with ctx:
        def sb(name, shape, dt=f32):
            return ctx.enter_context(nc.sbuf_tensor(name, shape, dt))

        def sem(name):
            return ctx.enter_context(nc.semaphore(name))

        x = sb("x", [P, TT, D])
        awq, awk, awv, awo = (sb(n, [P, D]) for n in ("awq", "awk", "awv", "awo"))
        bwq, bwd, bwk = sb("bwq", [P, H * HD]), sb("bwd", [P, LR]), sb("bwk", [LR, H * HD])
        bwv, bwo = sb("bwv", [LR, H * HD]), sb("bwo", [P, HG, D])
        wi, wo = sb("wi", [P, F]), sb("wo", [P, FT, D])
        la, lb = sb("la", [ER, D]), sb("lb", [ER, F])
        idx_i, rowx = sb("idx_i", [ER, E2], i32), sb("rowx", [ER, 1])
        tv = sb("tv", [P, E2])
        ident, zero16 = sb("ident", [P, P]), sb("zero16", [P, BK], f16)
        ones = sb("ones", [P, HD])
        idx_f, pick = sb("idx_f", [ER, E2]), sb("pick", [ER, E2])
        lbx = sb("lbx", [ER, E2, F])
        weff = sb("weff", [P, E2, F])
        stats, mean = sb("stats", [P, TT, 6]), sb("mean", [P, TT])
        std, rstd = sb("std", [P, TT]), sb("rstd", [P, TT])
        diff, shift = sb("diff", [P, TT]), sb("shift", [P, TT])
        wide = sb("wide", [P, 2, N])
        h = wide[:, 0, :].rearrange("p (t d) -> p t d", d=D)
        hT = wide[:, 1, :]
        cmat, t1, zs = sb("cmat", [P, D]), sb("t1", [P, D]), sb("zs", [P, D])
        zmax, zsum, zrec = sb("zmax", [P, 1]), sb("zsum", [P, 1]), sb("zrec", [P, 1])
        ze, zn = sb("ze", [P, D]), sb("zn", [P, D])
        ntm, mix = sb("ntm", [P, D]), sb("mix", [P, D])
        r0, r1 = sb("r0", [P, 2, BK]), sb("r1", [P, 2, BK])
        r = sb("r", [P, FT, BK])
        latT = sb("latT", [LR, N])
        high, low = sb("high", [P, 2 * HG, N], f16), sb("low", [P, 2 * HG, N], f16)
        Qs, Ks = sb("Qs", [P, NCH, H, QC], f16), sb("Ks", [P, H, N], f16)
        V = sb("V", [P, KB, H * HD])
        vst = sb("vst", [P, HG, 2, P])
        prob = high[:, :, :].bitcast(f32).rearrange("p s (h q) -> p (s h) q", q=QC).rearrange("p (k h) q -> p k h q", k=2)
        pair = low[:, 0:2, :].bitcast(f32).rearrange("p s (h q) -> p (s h) q", q=QC)
        mpart, mcol = sb("mpart", [P, H, U]), sb("mcol", [P, H * QT])
        mh, ml = sb("mh", [H * QT, P], f16), sb("ml", [H * QT, P], f16)
        oraw, osum, orec = sb("oraw", [P, BK]), sb("osum", [P, BK]), sb("orec", [P, BK])
        oT = wide

        ps = ctx.enter_context(nc.psum_tensor("ps", [P, 8, BK], f32))
        MB0, EB0, OB, SB = 0, NM, NM + NE, NM + NE + 1

        HB0, YB = 4, 0

        s_in = [sem(f"s_in{b}") for b in range(NB)]
        s_wa, s_wf, s_wb, s_out = (sem(n) for n in ("s_wa", "s_wf", "s_wb", "s_out"))
        s_gp, s_dv, s_shift = sem("s_gp"), sem("s_dv"), sem("s_shift")
        s_const, s_pick, s_weffp, s_weff = sem("s_const"), sem("s_pick"), sem("s_weffp"), sem("s_weff")
        s_st, s_ve = sem("s_st"), sem("s_ve")
        s_std, s_h, s_tr, s_hT = sem("s_std"), sem("s_h"), sem("s_tr"), sem("s_hT")
        s_ap, s_az, s_am = sem("s_ap"), sem("s_az"), sem("s_am")
        s_ze, s_mask = sem("s_ze"), sem("s_mask")
        s_mixp, s_x1 = sem("s_mixp"), sem("s_x1")
        s_hid, s_r0, s_r1, s_r, s_dn, s_xf = (sem(n) for n in ("s_hid", "s_r0", "s_r1", "s_r", "s_dn", "s_xf"))
        s_lat, s_latc, s_qk, s_hi, s_lo, s_vp, s_vc = (sem(n) for n in ("s_lat", "s_latc", "s_qk", "s_hi", "s_lo", "s_vp", "s_vc"))
        s_stack, s_lows, s_ones = [sem(f"s_stack{g}") for g in range(HG)], sem("s_lows"), sem("s_ones")
        s_sm, s_maxed, s_mcol, s_mT, s_mneg, s_mrow = (sem(n) for n in ("s_sm", "s_maxed", "s_mcol", "s_mT", "s_mneg", "s_mrow"))
        s_se, s_p, s_pv, s_pair, s_sum, s_vst = (sem(n) for n in ("s_se", "s_p", "s_pv", "s_pair", "s_sum", "s_vst"))
        s_evac, s_orec, s_oT = sem("s_evac"), sem("s_orec"), sem("s_oT")
        s_norm = sem("s_norm")
        s_wop, s_x3 = sem("s_wop"), sem("s_x3")

        block = ctx.enter_context(nc.Block())
        K_HIGH, K_LOW, Q_HIGH, Q_LOW = (0, 2), 1, (0, 1), 2

        def stack_of(n, row, hd):
            rows = slice(row * HD, (row + 1) * HD)
            return Qs[rows, :, hd, :] if n else Ks[rows, hd, :]

        nat = lambda t: t.rearrange("(t p) d -> p t d", p=P)

        @block.sync
        def _(sp):
            for b in range(NB):
                sp.dma_start(x[:, b * TB:(b + 1) * TB, :], nat(x_in)[:, b * TB:(b + 1) * TB, :]).then_inc(s_in[b], 16)
            for dst, src in ((awk, a_wkT), (awq, a_wqT), (awv, a_wv), (awo, a_woT)):
                sp.dma_start(dst[:, :], src).then_inc(s_wa, 16)
            for dst, src in ((bwq, b_wqT), (bwd, b_wdT), (bwk, b_wkT), (bwv, b_wvT)):
                sp.dma_start(dst[:, :], src).then_inc(s_wb, 16)
            sp.dma_start(bwo[:, :, :], b_woT.rearrange("(g p) d -> p g d", p=P)).then_inc(s_wb, 16)

            for g in range(HG):
                for n, (stack, rows) in enumerate(((Ks, K_HIGH), (Qs, Q_HIGH))):
                    slot = 2 * g + n
                    sp.wait_ge(s_hi, NB * (slot + 1))
                    for hh in range(HPG):
                        for row in rows:
                            dst = stack_of(n, row, HPG * g + hh)
                            src = high[hh * HD:(hh + 1) * HD, slot, :]
                            if n:
                                src = src.rearrange("r (c q) -> r c q", q=QC)
                            sp.dma_start(dst, src).then_inc(s_stack[g], 16)

            def max_rows(chunk):
                sp.wait_ge(s_mneg, 2 * chunk + 2)
                for row, part in ((SK, mh), (SK + 1, ml)):
                    dst = Qs[row:row + 1, ds(chunk, 1), :, :].rearrange("o c h q -> o (c h q)")
                    sp.dma_start(dst, part[:, :]).then_inc(s_mrow, 16)

            max_rows(0)
            with sp.Fori(0, NCH - 1) as c:
                max_rows(c + 1)
            for b in range(NB):
                sp.wait_ge(s_xf, NB + b + 2)
                sp.dma_start(nat(out)[:, b * TB:(b + 1) * TB, :], x[:, b * TB:(b + 1) * TB, :]).then_inc(s_out, 16)
            sp.wait_ge(s_out, 16 * NB)

        @block.gpsimd
        def _(gp):
            gp.memset(ident[:, :], 0.0).then_inc(s_gp, 1)
            gp.wait_ge(s_gp, 1)
            gp.affine_select(out=ident[:, :], in_=ident[:, :], compare_op=ALU.not_equal, fill=1.0,
                             base=0, pattern=[[-1, P]], channel_multiplier=1).then_inc(s_const, 1)
            gp.memset(ones[:, :], 1.0).then_inc(s_const, 1)
            gp.memset(zero16[:, :], 0.0).then_inc(s_const, 1)
            gp.wait_ge(s_const, 3)
            gp.memset(Ks[SK:SR, :, :], 1.0).then_inc(s_ones, 1)
            gp.wait_ge(s_ones, 1)
            gp.wait_ge(s_az, 3)
            blocks = zs[:, :].rearrange("p (b j) -> p b j", j=AD)
            gp.affine_select(out=blocks, in_=blocks, compare_op=ALU.is_ge, fill=-1e30, base=0,
                             pattern=[[-AD, A_HEADS], [0, AD]], channel_multiplier=1).then_inc(s_gp, 1)
            gp.wait_ge(s_gp, 2)
            gp.affine_select(out=blocks, in_=blocks, compare_op=ALU.is_ge, fill=-1e30, base=AD - 1,
                             pattern=[[AD, A_HEADS], [0, AD]], channel_multiplier=-1).then_inc(s_mask, 1)

            gp.wait_ge(s_lows, 2 * HG)
            gp.sem_inc(s_pair, HG)
            with gp.Fori(0, NCH) as c:
                with gp.Fori(0, KP) as p:
                    n = c * KP + p
                    for g in range(HG):
                        gp.wait_ge(s_p, n * U + (NE + 4 * g + 4))
                        gp.wait_ge(s_sum, n * HG + (g + 1))
                        hs = slice(g * HPG, (g + 1) * HPG)
                        gp.tensor_tensor(pair[:, hs, :], prob[:, 0, hs, :], prob[:, 1, hs, :],
                                         ALU.add).then_inc(s_pair, 1)

        @block.scalar
        def _(act):
            for dst, src in ((la, lora_a), (lb, lora_bT), (wi, wiT)):
                act.dma_start(dst[:, :], src).then_inc(s_wf, 16)
            act.dma_start(wo[:, :, :], woT.rearrange("(t p) d -> p t d", p=P)).then_inc(s_wf, 16)
            act.dma_start(rowx[:, :], row_expert).then_inc(s_wf, 16)
            act.dma_start(idx_i[:, :], top_idx.partition_broadcast(ER)).then_inc(s_wf, 16)
            act.dma_start(tv[:, :], top_val.partition_broadcast(P)).then_inc(s_wf, 16)

            def ln(k):
                act.wait_ge(s_ve, k + 1)
                act.activation(std[:, :], std[:, :], ACT.Sqrt).then_inc(s_std, 1)
                act.wait_ge(s_shift, k + 1)
                for t in range(TT // 2, TT):
                    act.activation(h[:, t, :], x[:, t, :], ACT.Identity, bias=shift[:, t:t + 1],
                                   scale=rstd[:, t:t + 1]).then_inc(s_norm, 1)
                for b in range(NB // 2, NB):
                    act.wait_ge(s_tr, NB * k + b + 1)
                    act.wait_ge(s_hT, NB * k + b)
                    act.copy(hT[:, b * BK:(b + 1) * BK], ps[:, b, :]).then_inc(s_hT, 1)

            def ffn(k):
                with act.Fori(0, NB) as c:
                    for ft in range(FT):
                        act.wait_ge(s_hid, c * FT + (k * NB * FT + ft + 1))
                        act.wait_ge(s_r, c * FT + (k * NB * FT + ft + 1))
                        act.activation(r0[:, ft % 2, :], ps[:, HB0 + 2 * (ft % 2), :], ACT.Relu).then_inc(s_r0, 1)

            ln(0)
            act.wait_ge(s_am, 1)
            act.activation(ze[:, :], zs[:, :], ACT.Exp, bias=zmax[:, :], accum_out=zsum[:, :]).then_inc(s_ze, 1)
            ln(1)
            ffn(0)
            ln(2)
            for b in range(NB):
                act.wait_ge(s_lat, b + 1)
                act.copy(latT[:, b * BK:(b + 1) * BK], ps[0:LR, 4 + b, :]).then_inc(s_latc, 1)
            for n in range(2 * HG * NB):
                act.wait_ge(s_qk, n + 1)
                act.copy(high[:, n // NB, (n % NB) * BK:(n % NB + 1) * BK], ps[:, n % 4, :]).then_inc(s_hi, 1)
            for n in range(KB // 2):
                act.wait_ge(s_vp, n + 1)
                act.copy(V[:, 2 * n:2 * n + 2, :].rearrange("p a b -> p (a b)"), ps[:, 4 + n % 4, :]).then_inc(s_vc, 1)

            act.sem_inc(s_p, NE)
            act.preload_act_table(ACT.Exp)

            def exponentials(chunk, p, between=None):
                n = chunk * KP + p
                for u in range(U):
                    g, k, hp = u // 4, (u // 2) % 2, u % 2
                    if u % 4 == 0:
                        act.wait_ge(s_pair, n * HG + (g + 1))
                    if u % 2 == 0:
                        act.wait_ge(s_pv, n * 4 + (2 * g + k + 1))
                    if u % 4 == 2:
                        act.copy(vst[:, g, :, :], V[:, ds(p * 2, 2), g * P:(g + 1) * P]).then_inc(s_vst, 1)
                    act.wait_ge(s_se, n * U + (u + 1))
                    hs = slice(HPG * g + 2 * hp, HPG * g + 2 * hp + 2)
                    act.activation(prob[:, k, hs, :].rearrange("p a b -> p (a b)"), ps[:, EB0 + u % NE, :],
                                   ACT.Exp, scale=SCALE).then_inc(s_p, 1)
                    if between and u == SUM_SLOT:
                        between()

            def evacuate(chunk):
                act.wait_ge(s_sum, chunk * HG * KP + (HG * KP + HG))
                act.wait_ge(s_oT, chunk * HG + HG)
                act.copy(osum[:, :], ps[:, SB, :]).then_inc(s_evac, 1)
                act.copy(oraw[:, :], ps[:, OB, :]).then_inc(s_evac, 1)

            exponentials(0, 0)
            with act.Fori(0, NCH - 1) as c:
                with act.Fori(1, KP) as p:
                    exponentials(c, p)
                exponentials(c + 1, 0, lambda: evacuate(c))
            with act.Fori(1, KP) as p:
                exponentials(NCH - 1, p)
            evacuate(NCH - 1)
            ln(3)
            ffn(1)

        @block.vector
        def _(dve):
            chain = [0]

            def link(ins):
                chain[0] += 1
                ins.then_inc(s_dv, 1)
                dve.wait_ge(s_dv, chain[0])

            def statistics(b):
                for j in range(TB):
                    t = ds(b * TB + j, 1)
                    dve.bn_stats(stats[:, t, :], x[:, t, :]).then_inc(s_st, 1)

            def ln(k):
                dve.wait_ge(s_st, TT * (k + 1))
                even, odd = stats[:, :, 1], stats[:, :, 4]
                dve.tensor_tensor(mean[:, :], even, odd, ALU.add).then_inc(s_dv, 1)
                dve.tensor_tensor(std[:, :], stats[:, :, 2], stats[:, :, 5], ALU.add).then_inc(s_dv, 1)
                chain[0] += 2
                link(dve.tensor_tensor(diff[:, :], even, odd, ALU.subtract))
                dve.tensor_scalar(mean[:, :], mean[:, :], 0.5, None, ALU.mult).then_inc(s_dv, 1)
                chain[0] += 1
                link(dve.tensor_tensor(diff[:, :], diff[:, :], diff[:, :], ALU.mult))
                link(dve.scalar_tensor_tensor(std[:, :], diff[:, :], D / 4.0, std[:, :], ALU.mult, ALU.add))
                dve.tensor_scalar(std[:, :], std[:, :], 1.0 / D, EPS, ALU.mult, ALU.add).then_inc(s_ve, 1)
                dve.wait_ge(s_std, k + 1)
                link(dve.reciprocal(rstd[:, :], std[:, :]))
                dve.scalar_tensor_tensor(shift[:, :], mean[:, :], -1.0, rstd[:, :], ALU.mult, ALU.mult).then_inc(s_shift, 1)
                for t in range(TT // 2):
                    dve.tensor_scalar(h[:, t, :], x[:, t, :], mean[:, t:t + 1], rstd[:, t:t + 1],
                                      ALU.subtract, ALU.mult).then_inc(s_h, 1)
                for b in range(NB // 2):
                    dve.wait_ge(s_tr, NB * k + b + 1)
                    dve.tensor_copy(hT[:, b * BK:(b + 1) * BK], ps[:, b, :]).then_inc(s_hT, 1)

            def ffn(k):
                def mix_experts(c, ft):
                    n = c * FT + (k * NB * FT + ft)
                    dve.wait_ge(s_hid, n + 1)
                    dve.tensor_scalar(r1[:, ft % 2, :], ps[:, HB0 + 2 * (ft % 2) + 1, :], 0.0, tv[:, 1:2],
                                      ALU.max, ALU.mult).then_inc(s_r1, 1)
                    dve.wait_ge(s_r1, n + 1)
                    dve.wait_ge(s_r0, n + 1)
                    dve.wait_ge(s_dn, n + 1)
                    dve.scalar_tensor_tensor(r[:, ft, :], r0[:, ft % 2, :], tv[:, 0:1], r1[:, ft % 2, :],
                                             ALU.mult, ALU.add).then_inc(s_r, 1)

                def add_result(c):
                    dve.wait_ge(s_dn, c * FT + (k * NB * FT + 2 * FT))
                    xs = x[:, ds(c * TB, TB), :].rearrange("p a b -> p (a b)")
                    dve.tensor_tensor(xs, ps[:, YB, :], xs, ALU.add).then_inc(s_xf, 1)
                    if k == 0:
                        dve.wait_ge(s_xf, c + 2)
                        statistics(c)

                mix_experts(0, 0)
                with dve.Fori(0, NB - 1) as c:
                    for ft in range(1, FT):
                        mix_experts(c, ft)
                    mix_experts(c + 1, 0)
                    add_result(c)
                for ft in range(1, FT):
                    mix_experts(NB - 1, ft)
                add_result(NB - 1)

            for b in range(NB):
                dve.wait_ge(s_in[b], 16)
                statistics(b)
            ln(0)
            dve.wait_ge(s_wf, 16 * 7)
            link(dve.tensor_copy(idx_f[:, :], idx_i[:, :]))
            link(dve.tensor_scalar(pick[:, :], idx_f[:, :], rowx[:, 0:1], None, ALU.is_equal))
            for e in range(E2):
                dve.tensor_scalar(lbx[:, e, :], lb[:, :], pick[:, e:e + 1], None, ALU.mult).then_inc(s_pick, 1)
            for n, dst in enumerate((cmat, t1)):
                dve.wait_ge(s_ap, n + 1)
                dve.tensor_copy(dst[:, :], ps[:, 4 + n, 0:D]).then_inc(s_az, 1)
            dve.wait_ge(s_ap, 3)
            dve.tensor_scalar(zs[:, :], ps[:, 4, 0:D], float(AD) ** -0.5, None, ALU.mult).then_inc(s_az, 1)
            for e in range(E2):
                dve.wait_ge(s_weffp, e + 1)
                dve.tensor_tensor(weff[:, e, :], ps[:, 6 + e, :], wi[:, :], ALU.add).then_inc(s_weff, 1)
            dve.wait_ge(s_mask, 1)
            link(dve.reduce_max(zrec[:, :], zs[:, :], axis=AX))
            dve.tensor_scalar(zmax[:, :], zrec[:, :], -1.0, None, ALU.mult).then_inc(s_am, 1)
            dve.wait_ge(s_ze, 1)
            dve.wait_ge(s_am, 1)
            link(dve.reciprocal(zrec[:, :], zsum[:, :]))
            dve.tensor_scalar(zn[:, :], ze[:, :], zrec[:, 0:1], None, ALU.mult).then_inc(s_az, 1)
            for n, (dst, bank) in enumerate(((ntm, 5), (mix, 4))):
                dve.wait_ge(s_ap, n + 4)
                dve.tensor_copy(dst[:, :], ps[:, bank, 0:D]).then_inc(s_az, 1)
            for b in range(NB):
                dve.wait_ge(s_mixp, b + 1)
                xs = x[:, b * TB:(b + 1) * TB, :].rearrange("p a b -> p (a b)")
                dve.tensor_tensor(xs, ps[:, b, :], xs, ALU.add).then_inc(s_x1, 1)
                dve.wait_ge(s_x1, b + 1)
                statistics(b)
            dve.sem_inc(s_r, 2)
            ln(1)
            ffn(0)
            ln(2)
            for n in range(2 * HG * NB):
                cols = slice((n % NB) * BK, (n % NB + 1) * BK)
                dve.wait_ge(s_hi, n + 1)
                dve.tensor_tensor(low[:, n // NB, cols], ps[:, n % 4, :], high[:, n // NB, cols],
                                  ALU.subtract).then_inc(s_lo, 1)
                if n % NB == NB - 1:
                    slot = n // NB
                    g, of_q = slot // 2, slot % 2
                    dve.wait_ge(s_lo, n + 1)
                    for hh in range(HPG):
                        dst = stack_of(of_q, Q_LOW if of_q else K_LOW, HPG * g + hh)
                        src = low[hh * HD:(hh + 1) * HD, slot, :]
                        if of_q:
                            src = src.rearrange("r (c q) -> r c q", q=QC)
                        last = dve.tensor_copy(dst, src)
                    last.then_inc(s_lows, 1)

            dve.sem_inc(s_maxed, NM)
            dve.sem_inc(s_oT, HG)

            def maxima(chunk, hd, units=range(U)):
                for u in units:
                    dve.wait_ge(s_sm, chunk * H * U + (hd * U + (u + 1)))
                    dve.reduce_max(mpart[:, ds(hd, 1), u:u + 1], ps[:, MB0 + u % NM, :], axis=AX).then_inc(s_maxed, 1)

            def columns(chunk):
                dve.wait_ge(s_maxed, chunk * H * U + (H * U + NM))
                dve.reduce_max(mcol[:, :], mpart[:, :, :].rearrange("p h (t j) -> p (h t) j", t=QT),
                               axis=AX).then_inc(s_mcol, 1)
                dve.wait_ge(s_mcol, chunk + 1)

            def split(chunk):
                dve.wait_ge(s_mT, chunk + 1)
                dve.wait_ge(s_mrow, chunk * MROW)
                mT = ps[0:H * QT, MB0 + 2 % NM, 0:P]
                dve.tensor_scalar(mh[:, :], mT, -1.0, None, ALU.mult).then_inc(s_mneg, 1)
                dve.wait_ge(s_mneg, chunk * 2 + 1)
                dve.scalar_tensor_tensor(ml[:, :], mT, -1.0, mh[:, :], ALU.mult, ALU.subtract).then_inc(s_mneg, 1)

            RP = BK // U

            def reciprocals(chunk, piece):
                dve.wait_ge(s_evac, chunk * 2 + 3)
                dve.reciprocal(orec[:, ds(piece * RP, RP)], osum[:, ds(piece * RP, RP)]).then_inc(s_orec, 1)

            def normalise(chunk):
                dve.wait_ge(s_evac, chunk * 2 + 4)
                dve.wait_ge(s_orec, chunk * U + U)
                for g in range(HG):
                    dve.tensor_tensor(oT[:, g, ds(chunk * QC, QC)], oraw[:, g * QC:(g + 1) * QC],
                                      orec[:, g * QC:(g + 1) * QC], ALU.mult).then_inc(s_oT, 1)

            def with_maxima(c, of_last):
                with dve.Fori(2, H) as hd:
                    maxima(c + 1, hd)
                    if of_last:
                        reciprocals(c - 1, hd - 2)
                columns(c + 1)
                maxima(c + 2, 0, range(0, 2))
                split(c + 1)
                maxima(c + 2, 0, range(2, U))
                if of_last:
                    reciprocals(c - 1, H - 2)
                    reciprocals(c - 1, H - 1)
                    normalise(c - 1)
                maxima(c + 2, 1)

            with dve.Fori(0, H) as hd:
                maxima(0, hd)
            columns(0)
            maxima(1, 0, range(0, 2))
            split(0)
            maxima(1, 0, range(2, U))
            maxima(1, 1)
            with_maxima(0, False)
            with dve.Fori(1, NCH - 1) as c:
                with_maxima(c, True)
            for chunk in (NCH - 2, NCH - 1):
                for piece in range(U):
                    reciprocals(chunk, piece)
                normalise(chunk)
            for b in range(NB):
                dve.wait_ge(s_wop, b + 1)
                xs = x[:, b * TB:(b + 1) * TB, :].rearrange("p a b -> p (a b)")
                dve.tensor_tensor(xs, ps[:, b, :], xs, ALU.add).then_inc(s_x3, 1)
                dve.wait_ge(s_x3, b + 1)
                statistics(b)
            ln(3)
            ffn(1)

        @block.tensor
        def _(pe):
            mm = pe.matmul

            def transposed(k, then=None):
                for b in range(NB):
                    half = NB // 2
                    if b < half:
                        pe.wait_ge(s_h, TT // 2 * k + (b + 1) * TB)
                    else:
                        pe.wait_ge(s_norm, TT // 2 * k + (b - half + 1) * TB)
                    for t in range(TB):
                        last = pe.transpose(ps[:, b, t * P:(t + 1) * P], h[:, b * TB + t, :], ident[:, :])
                    last.then_inc(s_tr, 1)
                    if then:
                        then(b)

            def ffn(k):
                def hidden(c, ft):
                    pe.wait_ge(s_hT, c + (k * 2 * NB + NB + 1))
                    pe.wait_ge(s_r, c * FT + (k * NB * FT + ft + 1))
                    for e in range(E2):
                        last = mm(ps[:, HB0 + 2 * (ft % 2) + e, :], weff[:, e, ft * P:(ft + 1) * P],
                                  hT[:, ds(c * BK, BK)], start=True, stop=True)
                    last.then_inc(s_hid, 1)

                def down(c, ft):
                    pe.wait_ge(s_r, c * FT + (k * NB * FT + ft + 3))
                    if ft == 0:
                        pe.wait_ge(s_xf, c + (k * NB + 1))
                    for t in range(TB):
                        last = mm(ps[:, YB, t * P:(t + 1) * P], r[:, ft, t * P:(t + 1) * P], wo[:, ft, :],
                                  start=(ft == 0 and t == 0), stop=(ft == FT - 1), skip_group_check=True)
                    last.then_inc(s_dn, 1)

                def chunk(c, more):
                    for ft in range(1, FT):
                        hidden(c, ft)
                        down(c, ft - 1)
                    if more:
                        hidden(c + 1, 0)
                    down(c, FT - 1)

                hidden(0, 0)
                with pe.Fori(0, NB - 1) as c:
                    chunk(c, True)
                chunk(NB - 1, False)

            pe.wait_ge(s_const, 3)

            def lora(e):
                pe.wait_ge(s_pick, e + 1)
                mm(ps[:, 6 + e, :], la[:, :], lbx[:, e, :], start=True, stop=True).then_inc(s_weffp, 1)

            def gram(b):
                for t in range(b * TB, (b + 1) * TB):
                    last = mm(ps[:, 4, 0:D], h[:, t, :], h[:, t, :], start=(t == 0), stop=(t == TT - 1))
                if b == NB - 1:
                    last.then_inc(s_ap, 1)

            transposed(0, gram)
            pe.wait_ge(s_wa, 64)
            pe.wait_ge(s_az, 1)
            mm(ps[:, 5, 0:D], cmat[:, :], awk[:, :], start=True, stop=True).then_inc(s_ap, 1)
            lora(0)
            pe.wait_ge(s_az, 2)
            mm(ps[:, 4, 0:D], t1[:, :], awq[:, :], start=True, stop=True).then_inc(s_ap, 1)
            lora(1)
            pe.wait_ge(s_az, 4)
            mm(ps[:, 5, 0:D], zn[:, :], awv[:, :], start=True, stop=True).then_inc(s_ap, 1)
            pe.wait_ge(s_az, 5)
            mm(ps[:, 4, 0:D], ntm[:, :], awo[:, :], start=True, stop=True).then_inc(s_ap, 1)
            pe.wait_ge(s_az, 6)
            pe.wait_ge(s_hT, NB)
            for b in range(NB):
                for t in range(b * TB, (b + 1) * TB):
                    last = mm(ps[:, b, (t % TB) * P:(t % TB + 1) * P], hT[:, t * P:(t + 1) * P], mix[:, :],
                              start=True, stop=True)
                last.then_inc(s_mixp, 1)
            pe.wait_ge(s_x1, NB)
            pe.sem_inc(s_dn, FT)
            pe.wait_ge(s_weff, E2)
            pe.sem_inc(s_xf, 1)
            transposed(1)
            ffn(0)
            pe.wait_ge(s_xf, NB + 1)
            transposed(2)
            pe.wait_ge(s_hT, 3 * NB)
            pe.wait_ge(s_wb, 16 * 5)
            for b in range(NB):
                mm(ps[0:LR, 4 + b, :], bwd[:, :], hT[:, b * BK:(b + 1) * BK], start=True, stop=True).then_inc(s_lat, 1)
            pe.wait_ge(s_latc, NB)
            for n in range(2 * HG * NB):
                slot, b = n // NB, n % NB
                g, of_q = slot // 2, slot % 2
                w, rhs = (bwq, hT) if of_q else (bwk, latT)
                if n >= 4:
                    pe.wait_ge(s_lo, n - 3)
                mm(ps[:, n % 4, :], w[:, g * P:(g + 1) * P], rhs[:, b * BK:(b + 1) * BK],
                   start=True, stop=True).then_inc(s_qk, 1)
            for n in range(KB // 2):
                if n >= 4:
                    pe.wait_ge(s_vc, n - 3)
                for k in range(2):
                    kb = 2 * n + k
                    last = mm(ps[:, 4 + n % 4, k * H * HD:(k + 1) * H * HD], latT[:, kb * P:(kb + 1) * P], bwv[:, :],
                              start=True, stop=True)
                last.then_inc(s_vp, 1)
            pe.wait_ge(s_vc, KB // 2)
            pe.wait_ge(s_lo, 2 * HG * NB)
            pe.sem_inc(s_pv, 4)
            pe.sem_inc(s_sum, HG)
            pe.sem_inc(s_evac, 2)

            def score_max(chunk, hd, u):
                t, j = u // 4, u % 4
                pe.wait_ge(s_maxed, chunk * H * U + (hd * U + (u + 1)))
                at = chunk if isinstance(chunk, int) else chunk % NCH
                mm(ps[:, MB0 + u % NM, :], Qs[0:SK, ds(at, 1), ds(hd, 1), t * P:(t + 1) * P],
                   Ks[0:SK, ds(hd, 1), j * BK:(j + 1) * BK], start=True, stop=True).then_inc(s_sm, 1)

            def max_transpose(chunk):
                pe.wait_ge(s_mcol, chunk + 1)
                pe.wait_ge(s_maxed, chunk * H * U + (H * U + 3))
                pe.transpose(ps[0:H * QT, MB0 + 2 % NM, 0:P], mcol[:, :], ident[:, :]).then_inc(s_mT, 1)

            def score_exp(chunk, p, u):
                g, k, hp = u // 4, (u // 2) % 2, u % 2
                pe.wait_ge(s_p, (chunk * KP + p) * U + (u + 1))
                for a in range(2):
                    hd = HPG * g + 2 * hp + a
                    last = mm(ps[:, EB0 + u % NE, a * QC:(a + 1) * QC], Ks[0:SR, hd, ds(p * 2 * P + k * P, P)],
                              Qs[0:SR, ds(chunk, 1), hd, :], start=True, stop=True)
                last.then_inc(s_se, 1)

            def weigh(n, g, k):
                if k == 0:
                    pe.wait_ge(s_vst, n * HG + (g + 1))
                pe.wait_ge(s_p, n * U + (NE + 4 * g + 2 * k + 2))
                for j in range(HPG):
                    last = mm(ps[j * HD:(j + 1) * HD, OB, g * QC:(g + 1) * QC], vst[:, g, k, j * HD:(j + 1) * HD],
                              prob[:, k, HPG * g + j, :], start=False, stop=True, skip_group_check=True)
                last.then_inc(s_pv, 1)

            def total(n, g):
                pe.wait_ge(s_pair, n * HG + (HG + g + 1))
                for j in range(HPG):
                    last = mm(ps[j * HD:(j + 1) * HD, SB, g * QC:(g + 1) * QC], ones[:, :], pair[:, HPG * g + j, :],
                              start=False, stop=True, skip_group_check=True)
                last.then_inc(s_sum, 1)

            def clear(chunk):
                pe.wait_ge(s_evac, chunk * 2 + 2)
                for bank in (OB, SB):
                    mm(ps[:, bank, :], zero16[:, 0:P], zero16[:, :], start=True, stop=True)

            def first(chunk, head_of, rest):
                n = chunk * KP
                pe.wait_ge(s_mrow, chunk * MROW + MROW)
                for u in range(U):
                    score_max(*head_of, u)
                    score_exp(chunk, 0, u)
                    if rest and u == 1:
                        weigh(n - 1, 1, 1)
                    if rest and u == 2:
                        total(n - 1, 0)
                    if rest and u == SUM_SLOT:
                        total(n - 1, 1)
                clear(chunk)
                for g, k in ((0, 0), (0, 1), (1, 0)):
                    weigh(n, g, k)

            def pair_of_blocks(chunk, p, head_of=None, transpose=False):
                n = chunk * KP + p
                units = list(range(U))
                for u in range(U):
                    if transpose and u == 2:
                        max_transpose(chunk + 1)
                    elif head_of:
                        if transpose and u == 3:
                            pe.wait_ge(s_mneg, chunk * 2 + 4)
                        score_max(*head_of, units.pop(0))
                    score_exp(chunk, p, u)
                    if u == 1:
                        weigh(n - 1, 1, 1)
                    if u == 2:
                        total(n - 1, 0)
                    if u == 3:
                        weigh(n, 0, 0)
                    if u == 5:
                        weigh(n, 0, 1)
                    if u == 6:
                        total(n - 1, 1)
                    if u == 7:
                        weigh(n, 1, 0)
                    if transpose and u == 6:
                        score_max(*head_of, units.pop(0))

            for g in range(HG):
                pe.wait_ge(s_stack[g], 16 * 4 * HPG)
                pe.wait_ge(s_lows, 2 * (g + 1))
                with pe.Fori(g * HPG, (g + 1) * HPG) as hd:
                    for u in range(U):
                        score_max(0, hd, u)
            for u in range(U):
                if u == 2:
                    max_transpose(0)
                    pe.wait_ge(s_mneg, 2)
                score_max(1, 0, u)
            first(0, (1, 1), False)
            with pe.Fori(0, NCH - 1) as c:
                with pe.Fori(1, KP - 1) as p:
                    pair_of_blocks(c, p, (c + 1, p + 1))
                pair_of_blocks(c, KP - 1, (c + 2, 0), True)
                first(c + 1, (c + 2, 1), True)
            with pe.Fori(1, KP) as p:
                pair_of_blocks(NCH - 1, p)
            n = NCH * KP
            weigh(n - 1, 1, 1)
            total(n - 1, 0)
            total(n - 1, 1)

            pe.wait_ge(s_maxed, (NCH * H + 2) * U + NM)
            for b in range(NB):
                pe.wait_ge(s_oT, HG * ((b + 1) * BK // QC + 1))
                for t in range(b * TB, (b + 1) * TB):
                    for g in range(HG):
                        last = mm(ps[:, b, (t % TB) * P:(t % TB + 1) * P], oT[:, g, t * P:(t + 1) * P], bwo[:, g, :],
                                  start=(g == 0), stop=(g == HG - 1))
                last.then_inc(s_wop, 1)
            transposed(3)
            ffn(1)


def kernel(**inputs):
    import concourse.bacc as bacc
    from concourse.bass_utils import run_bass_kernel_spmd

    a = {k: np.asarray(v) for k, v in inputs.items()}
    T = lambda v: np.ascontiguousarray(v.T)
    x = a["L0_attn_a_x"]
    experts, rank, d = a["L0_ffn_lora_As"].shape
    f = a["L0_ffn_lora_Bs"].shape[1]
    arrays = {
        "x_in": np.ascontiguousarray(x.reshape(-1, d)),
        "a_wqT": T(a["L0_attn_a_Wq"]), "a_wkT": T(a["L0_attn_a_Wk"]),
        "a_wv": np.ascontiguousarray(a["L0_attn_a_Wv"]), "a_woT": T(a["L0_attn_a_Wo"]),
        "b_wqT": T(a["L0_attn_b_Wq"]), "b_wdT": T(a["L0_attn_b_Wkv_down"]),
        "b_wkT": T(a["L0_attn_b_Wk_up"]), "b_wvT": T(a["L0_attn_b_Wv_up"]), "b_woT": T(a["L0_attn_b_Wo"]),
        "wiT": T(a["L0_ffn_wi_w"]), "woT": T(a["L0_ffn_wo_w"]),
        "lora_a": np.ascontiguousarray(a["L0_ffn_lora_As"].reshape(experts * rank, d)),
        "lora_bT": np.ascontiguousarray(a["L0_ffn_lora_Bs"].transpose(0, 2, 1).reshape(experts * rank, f)),
        "top_idx": np.ascontiguousarray(a["L0_ffn_top_k_indices"]),
        "top_val": np.ascontiguousarray(a["L0_ffn_top_k_values"]),
        "row_expert": np.repeat(np.arange(experts, dtype=np.float32), rank)[:, None],
    }
    nc = bacc.Bacc("TRN2", target_bir_lowering=False, num_devices=1)
    aps = [nc.dram_tensor(k, v.shape, mybir.dt.from_np(v.dtype), kind="ExternalInput").ap() for k, v in arrays.items()]
    out = nc.dram_tensor("out", arrays["x_in"].shape, mybir.dt.float32, kind="ExternalOutput").ap()
    build(nc, *aps, out)
    r = run_bass_kernel_spmd(nc, [arrays], core_ids=[0])
    return r.results[0]["out"].reshape(x.shape)
```

```python
import numpy as np
import concourse.bass as bass
from concourse import mybir
from contextlib import ExitStack



def build(nc, x_in, a_wqT, a_wkT, a_wv, a_woT, b_wqT, b_wdT, b_wkT, b_wvT, b_woT,
          wiT, woT, lora_a, lora_bT, top_idx, top_val, row_expert, out):
    f32, f16, i32 = mybir.dt.float32, mybir.dt.float16, mybir.dt.int32
    ALU, ACT, AX = mybir.AluOpType, mybir.ActivationFunctionType, mybir.AxisListType.X
    ds = bass.ds

    P = 128
    N, D = x_in.shape
    TT = N // P
    BK = 512
    TB = BK // P
    NB = TT // TB
    EPS = 1e-5
    A_HEADS = 16
    AD = D // A_HEADS
    H, HD, LR = 8, 32, b_wdT.shape[1]
    HPG = 4
    HG = 2
    SCALE = float(HD) ** -0.5
    QC = 256
    NCH = N // QC
    QT = QC // P
    KB = N // P
    KP = KB // 2
    SK = 3 * HD
    MROW = 16 * 2
    SR = SK + 2
    U = 8
    KQ = KP // 2
    NM, NE = 4, 2
    F = wiT.shape[1]
    FT = F // P
    E2 = 2
    OF_FFN = 1, 3
    ER = lora_a.shape[0]

    ctx = ExitStack()
    with ctx:
        def sb(name, shape, dt=f32):
            return ctx.enter_context(nc.sbuf_tensor(name, shape, dt))

        def sem(name):
            return ctx.enter_context(nc.semaphore(name))

        x = sb("x", [P, TT, D])
        awq, awk, awv, awo = (sb(n, [P, D]) for n in ("awq", "awk", "awv", "awo"))
        bwq, bwd, bwk = sb("bwq", [P, H * HD]), sb("bwd", [P, LR]), sb("bwk", [LR, H * HD])
        bwv, bwo = sb("bwv", [LR, H * HD]), sb("bwo", [P, HG, D])
        wi, wo = sb("wi", [P, F]), sb("wo", [P, FT, D])
        la, lb = sb("la", [ER, D]), sb("lb", [ER, F])
        idx_i, rowx = sb("idx_i", [ER, E2], i32), sb("rowx", [ER, 1])
        tv = sb("tv", [P, E2])
        ident, zero16 = sb("ident", [P, P]), sb("zero16", [P, BK], f16)
        ones = sb("ones", [P, HD])
        idx_f, pick = sb("idx_f", [ER, E2]), sb("pick", [ER, E2])
        lbx = sb("lbx", [ER, E2, F])
        weff = sb("weff", [P, E2, F])
        wh, wl = sb("wh", [P, E2, F], f16), sb("wl", [P, E2, F], f16)
        stats, mean = sb("stats", [P, TT, 6]), sb("mean", [P, TT])
        std, rstd = sb("std", [P, TT]), sb("rstd", [P, TT])
        diff, shift = sb("diff", [P, TT]), sb("shift", [P, TT])
        wide = sb("wide", [P, 2, N])
        h = wide[:, 0, :].rearrange("p (t d) -> p t d", d=D)
        hT = wide[:, 1, :]
        hTh, hTl = (hT.bitcast(f16)[:, n * N:(n + 1) * N] for n in range(2))
        cmat, t1, zs = sb("cmat", [P, D]), sb("t1", [P, D]), sb("zs", [P, D])
        zmax, zsum, zrec = sb("zmax", [P, 1]), sb("zsum", [P, 1]), sb("zrec", [P, 1])
        ze, zn = sb("ze", [P, D]), sb("zn", [P, D])
        ntm, mix = sb("ntm", [P, D]), sb("mix", [P, D])
        work = sb("work", [P, (FT + 4) * BK])
        banks = work[:, :].rearrange("p (t n) -> p t n", n=BK)
        r, r0, r1 = banks[:, 0:FT, :], banks[:, FT:FT + 2, :], banks[:, FT + 2:FT + 4, :]
        latT = sb("latT", [LR, N])
        high, low = sb("high", [P, 2 * HG, N], f16), sb("low", [P, 2 * HG, N], f16)
        Qs, Ks = sb("Qs", [P, NCH, H, QC], f16), sb("Ks", [P, H, N], f16)
        V = sb("V", [P, KB, H * HD])
        vst = sb("vst", [P, HG, 2, P])
        prob = [half.rearrange("p (k h q) -> p k h q", k=2, q=QC)
                for half in (high[:, :, :].bitcast(f32).rearrange("p s n -> p (s n)"), work[:, :])]
        pair = low[:, :, :].bitcast(f32).rearrange("p s (h q) -> p (s h) q", q=QC).rearrange("p (k h) q -> p k h q", k=2)
        mpart, mcol = sb("mpart", [P, H, U]), sb("mcol", [P, H * QT])
        mh, ml = sb("mh", [H * QT, P], f16), sb("ml", [H * QT, P], f16)
        oraw, osum, orec = sb("oraw", [P, BK]), sb("osum", [P, BK]), sb("orec", [P, BK])
        lst = oraw[0:LR, 0:2 * P]
        oT = wide

        ps = ctx.enter_context(nc.psum_tensor("ps", [P, 8, BK], f32))
        MB0, EB0, OB, SB = 0, NM, NM + NE, NM + NE + 1

        VB = OB
        HB, YB = (6, 4, 2, 4), 0

        s_in = [sem(f"s_in{b}") for b in range(NB)]
        s_wa, s_wf, s_wb, s_out = (sem(n) for n in ("s_wa", "s_wf", "s_wb", "s_out"))
        s_gp, s_dv, s_shift = sem("s_gp"), sem("s_dv"), sem("s_shift")
        s_const, s_pick, s_weffp, s_weff = sem("s_const"), sem("s_pick"), sem("s_weffp"), sem("s_weff")
        s_st, s_ve = sem("s_st"), sem("s_ve")
        s_std, s_h, s_tr, s_hT = sem("s_std"), sem("s_h"), sem("s_tr"), sem("s_hT")
        s_hTh, s_wh, s_wsplit = sem("s_hTh"), sem("s_wh"), sem("s_wsplit")
        s_ap, s_az, s_am = sem("s_ap"), sem("s_az"), sem("s_am")
        s_ze, s_mask = sem("s_ze"), sem("s_mask")
        s_mixp, s_x1 = sem("s_mixp"), sem("s_x1")
        s_hid, s_r0, s_r1, s_r, s_dn, s_xf = (sem(n) for n in ("s_hid", "s_r0", "s_r1", "s_r", "s_dn", "s_xf"))
        s_lat, s_latc, s_qk, s_hi, s_lo, s_lst, s_vp, s_vc = (
            sem(n) for n in ("s_lat", "s_latc", "s_qk", "s_hi", "s_lo", "s_lst", "s_vp", "s_vc"))
        s_stack, s_lows = ([sem(f"{n}{g}") for g in range(HG)] for n in ("s_stack", "s_lows"))
        s_ones = sem("s_ones")
        s_sm, s_maxed, s_mcol, s_mT, s_mneg, s_mrow = (sem(n) for n in ("s_sm", "s_maxed", "s_mcol", "s_mT", "s_mneg", "s_mrow"))
        s_se, s_p, s_pv, s_vst = (sem(n) for n in ("s_se", "s_p", "s_pv", "s_vst"))
        s_pair = [sem(f"s_pair{g}") for g in range(HG)]
        s_quad, s_sum = [sem(f"s_quad{g}") for g in range(HG)], [sem(f"s_sum{g}") for g in range(HG)]
        s_oraw, s_osum, s_orec, s_oT = (sem(n) for n in ("s_oraw", "s_osum", "s_orec", "s_oT"))
        s_norm = sem("s_norm")
        s_wop, s_x3 = sem("s_wop"), sem("s_x3")

        block = ctx.enter_context(nc.Block())
        K_HIGH, K_LOW, Q_HIGH, Q_LOW = (0, 2), 1, (0, 1), 2

        def stack_of(n, row, hd):
            rows = slice(row * HD, (row + 1) * HD)
            return Qs[rows, :, hd, :] if n else Ks[rows, hd, :]

        def sum_of_pair(engine, q, odd, g):
            engine.wait_ge(s_p, q * 2 * U + (odd * U + NE + 4 * g + 4))
            hs = slice(g * HPG, (g + 1) * HPG)
            engine.tensor_tensor(pair[:, odd, hs, :], prob[odd][:, 0, hs, :], prob[odd][:, 1, hs, :],
                                 ALU.add).then_inc(s_pair[g], 1)

        def sum_of_four(engine, q, g):
            engine.wait_ge(s_pair[g], q * 2 + 4)
            hs = slice(g * HPG, (g + 1) * HPG)
            engine.tensor_tensor(pair[:, 1, hs, :], pair[:, 0, hs, :], pair[:, 1, hs, :], ALU.add).then_inc(s_quad[g], 1)

        nat = lambda t: t.rearrange("(t p) d -> p t d", p=P)

        @block.sync
        def _(sp):
            for b in range(NB):
                sp.dma_start(x[:, b * TB:(b + 1) * TB, :], nat(x_in)[:, b * TB:(b + 1) * TB, :]).then_inc(s_in[b], 16)
            for dst, src in ((awk, a_wkT), (awq, a_wqT), (awv, a_wv), (awo, a_woT)):
                sp.dma_start(dst[:, :], src).then_inc(s_wa, 16)
            for dst, src in ((bwq, b_wqT), (bwd, b_wdT), (bwk, b_wkT), (bwv, b_wvT)):
                sp.dma_start(dst[:, :], src).then_inc(s_wb, 16)
            sp.dma_start(bwo[:, :, :], b_woT.rearrange("(g p) d -> p g d", p=P)).then_inc(s_wb, 16)

            for g in range(HG):
                for n, (stack, rows) in enumerate(((Ks, K_HIGH), (Qs, Q_HIGH))):
                    slot = 2 * g + n
                    sp.wait_ge(s_hi, NB * (slot + 1))
                    for hh in range(HPG):
                        for row in rows:
                            dst = stack_of(n, row, HPG * g + hh)
                            src = high[hh * HD:(hh + 1) * HD, slot, :]
                            if n:
                                src = src.rearrange("r (c q) -> r c q", q=QC)
                            sp.dma_start(dst, src).then_inc(s_stack[g], 16)
            def max_rows(chunk):
                sp.wait_ge(s_mneg, 2 * chunk + 2)
                for row, part in ((SK, mh), (SK + 1, ml)):
                    dst = Qs[row:row + 1, ds(chunk, 1), :, :].rearrange("o c h q -> o (c h q)")
                    sp.dma_start(dst, part[:, :]).then_inc(s_mrow, 16)

            max_rows(0)
            with sp.Fori(0, NCH - 1) as c:
                max_rows(c + 1)
            for b in range(NB):
                sp.wait_ge(s_xf, NB + b + 2)
                sp.dma_start(nat(out)[:, b * TB:(b + 1) * TB, :], x[:, b * TB:(b + 1) * TB, :]).then_inc(s_out, 16)
            sp.wait_ge(s_out, 16 * NB)

        @block.gpsimd
        def _(gp):
            gp.memset(ident[:, :], 0.0).then_inc(s_gp, 1)
            gp.wait_ge(s_gp, 1)
            gp.affine_select(out=ident[:, :], in_=ident[:, :], compare_op=ALU.not_equal, fill=1.0,
                             base=0, pattern=[[-1, P]], channel_multiplier=1).then_inc(s_const, 1)
            gp.memset(ones[:, :], 1.0).then_inc(s_const, 1)
            gp.memset(zero16[:, :], 0.0).then_inc(s_const, 1)
            gp.wait_ge(s_const, 3)
            gp.memset(Ks[SK:SR, :, :], 1.0).then_inc(s_ones, 1)
            gp.wait_ge(s_ones, 1)
            gp.wait_ge(s_az, 3)
            blocks = zs[:, :].rearrange("p (b j) -> p b j", j=AD)
            gp.affine_select(out=blocks, in_=blocks, compare_op=ALU.is_ge, fill=-1e30, base=0,
                             pattern=[[-AD, A_HEADS], [0, AD]], channel_multiplier=1).then_inc(s_gp, 1)
            gp.wait_ge(s_gp, 2)
            gp.affine_select(out=blocks, in_=blocks, compare_op=ALU.is_ge, fill=-1e30, base=AD - 1,
                             pattern=[[AD, A_HEADS], [0, AD]], channel_multiplier=-1).then_inc(s_mask, 1)

            gp.wait_ge(s_weff, E2)
            gp.tensor_copy(wh[:, :, :], weff[:, :, :]).then_inc(s_wh, 1)
            gp.wait_ge(s_wh, 1)
            gp.tensor_tensor(wl[:, :, :], weff[:, :, :], wh[:, :, :], ALU.subtract).then_inc(s_wsplit, 1)

            for g in range(HG):
                for n in range(2):
                    slot = 2 * g + n
                    gp.wait_ge(s_lo, NB * (slot + 1))
                    for hh in range(HPG):
                        src = low[hh * HD:(hh + 1) * HD, slot, :]
                        if n:
                            src = src.rearrange("r (c q) -> r c q", q=QC)
                        gp.dma_start(stack_of(n, Q_LOW if n else K_LOW, HPG * g + hh), src).then_inc(s_lows[g], 16)

            for g in range(HG):
                gp.wait_ge(s_lows[g], 16 * 2 * HPG)
            for g in range(HG):
                gp.sem_inc(s_pair[g], 2)
                gp.sem_inc(s_quad[g], 1)

            def of_both(q):
                gp.wait_ge(s_quad[0], q + 1)
                sum_of_pair(gp, q, 0, 0)
                gp.wait_ge(s_quad[1], q + 1)
                sum_of_pair(gp, q, 0, 1)
                gp.wait_ge(s_sum[0], q + 1)
                sum_of_pair(gp, q, 1, 0)
                gp.wait_ge(s_sum[1], q + 1)
                sum_of_pair(gp, q, 1, 1)
                sum_of_four(gp, q, 0)

            with gp.Fori(0, (NCH - 1) * KQ) as q:
                of_both(q)
            def of_first_group(q, four):
                gp.wait_ge(s_quad[0], q + 1)
                sum_of_pair(gp, q, 0, 0)
                gp.wait_ge(s_sum[0], q + 1)
                sum_of_pair(gp, q, 1, 0)
                if four:
                    sum_of_four(gp, q, 0)

            with gp.Fori((NCH - 1) * KQ, NCH * KQ - 1) as q:
                of_first_group(q, True)
            of_first_group(NCH * KQ - 1, False)

        @block.scalar
        def _(act):
            for dst, src in ((la, lora_a), (lb, lora_bT), (wi, wiT)):
                act.dma_start(dst[:, :], src).then_inc(s_wf, 16)
            act.dma_start(wo[:, :, :], woT.rearrange("(t p) d -> p t d", p=P)).then_inc(s_wf, 16)
            act.dma_start(rowx[:, :], row_expert).then_inc(s_wf, 16)
            act.dma_start(idx_i[:, :], top_idx.partition_broadcast(ER)).then_inc(s_wf, 16)
            act.dma_start(tv[:, :], top_val.partition_broadcast(P)).then_inc(s_wf, 16)

            def ln(k):
                act.wait_ge(s_ve, k + 1)
                act.activation(std[:, :], std[:, :], ACT.Sqrt).then_inc(s_std, 1)
                act.wait_ge(s_shift, k + 1)
                for t in range(TT // 2, TT):
                    act.activation(h[:, t, :], x[:, t, :], ACT.Identity, bias=shift[:, t:t + 1],
                                   scale=rstd[:, t:t + 1]).then_inc(s_norm, 1)
                if k in OF_FFN:
                    for b in range(NB):
                        act.wait_ge(s_tr, NB * k + b + 1)
                        act.copy(hTh[:, b * BK:(b + 1) * BK], ps[:, b, :]).then_inc(s_hTh, 1)
                    return
                for b in range(NB // 2, NB):
                    act.wait_ge(s_tr, NB * k + b + 1)
                    act.wait_ge(s_hT, NB * k + b)
                    act.copy(hT[:, b * BK:(b + 1) * BK], ps[:, b, :]).then_inc(s_hT, 1)

            def ffn(k):
                with act.Fori(0, NB) as c:
                    for ft in range(FT):
                        act.wait_ge(s_hid, c * FT + (k * NB * FT + ft + 1))
                        act.wait_ge(s_r, c * FT + (k * NB * FT + ft + 3))
                        act.activation(r0[:, ft % 2, :], ps[:, HB[ft], :], ACT.Relu).then_inc(s_r0, 1)

            ln(0)
            act.wait_ge(s_am, 1)
            act.activation(ze[:, :], zs[:, :], ACT.Exp, bias=zmax[:, :], accum_out=zsum[:, :]).then_inc(s_ze, 1)
            ln(1)
            ffn(0)
            ln(2)
            for b in range(NB):
                act.wait_ge(s_lat, b + 1)
                act.copy(latT[:, b * BK:(b + 1) * BK], ps[0:LR, 4 + b, :]).then_inc(s_latc, 1)
            for n in range(2 * HG * NB):
                act.wait_ge(s_qk, n + 1)
                act.copy(high[:, n // NB, (n % NB) * BK:(n % NB + 1) * BK], ps[:, n % 4, :]).then_inc(s_hi, 1)
            with act.Fori(0, KP) as n:
                act.wait_ge(s_vp, n + 1)
                act.copy(lst, latT[:, ds(n * 2 * P, 2 * P)]).then_inc(s_lst, 1)
                act.wait_ge(s_vp, n + 2)
                act.copy(V[:, ds(n * 2, 2), :].rearrange("p a b -> p (a b)"), ps[:, VB, :]).then_inc(s_vc, 1)

            act.sem_inc(s_p, NE)
            act.preload_act_table(ACT.Exp)

            def exponentials(chunk, p, odd, between={}):
                n = chunk * KP + p
                for u in range(U):
                    g, k, hp = u // 4, (u // 2) % 2, u % 2
                    if u % 4 == 0:
                        act.wait_ge(s_pair[g], n + 1)
                    if u % 2 == 0:
                        act.wait_ge(s_pv, n * 4 + (2 * g + k + 1))
                    if u % 4 == 2:
                        act.wait_ge(s_pv, n * 4 + (2 * g + 6))
                        act.copy(vst[:, g, :, :], V[:, ds(p * 2, 2), g * P:(g + 1) * P]).then_inc(s_vst, 1)
                    act.wait_ge(s_se, n * U + (u + 1))
                    hs = slice(HPG * g + 2 * hp, HPG * g + 2 * hp + 2)
                    act.activation(prob[odd][:, k, hs, :].rearrange("p a b -> p (a b)"), ps[:, EB0 + u % NE, :],
                                   ACT.Exp, scale=SCALE).then_inc(s_p, 1)
                    if u in between:
                        between[u]()

            def take_values(chunk):
                act.wait_ge(s_pv, chunk * KP * 4 + (KP * 4 + 8))
                act.wait_ge(s_oT, chunk * HG + HG)
                act.copy(oraw[:, :], ps[:, OB, :]).then_inc(s_oraw, 1)

            def take_sums(chunk):
                for g in range(HG):
                    act.wait_ge(s_sum[g], chunk * KQ + (KQ + 1))
                act.wait_ge(s_orec, chunk * U + 1)
                act.copy(osum[:, :], ps[:, SB, :]).then_inc(s_osum, 1)

            def rest_of_chunk(chunk, of_last):
                exponentials(chunk, 1, 1, {3: lambda: take_sums(chunk - 1)} if of_last else {})
                exponentials(chunk, 2, 0)
                with act.Fori(1, KQ - 1) as i:
                    exponentials(chunk, i * 2 + 1, 1)
                    exponentials(chunk, i * 2 + 2, 0)
                exponentials(chunk, KP - 1, 1)

            exponentials(0, 0, 0)
            rest_of_chunk(0, False)
            with act.Fori(1, NCH) as c:
                exponentials(c, 0, 0, {2: lambda: take_values(c - 1)})
                rest_of_chunk(c, True)
            ln(3)
            ffn(1)

        @block.vector
        def _(dve):
            chain = [0]

            def link(ins):
                chain[0] += 1
                ins.then_inc(s_dv, 1)
                dve.wait_ge(s_dv, chain[0])

            def statistics(b, tiles=range(TB)):
                for j in tiles:
                    t = ds(b * TB + j, 1)
                    dve.bn_stats(stats[:, t, :], x[:, t, :]).then_inc(s_st, 1)

            def ln(k):
                dve.wait_ge(s_st, TT * (k + 1))
                even, odd = stats[:, :, 1], stats[:, :, 4]
                dve.tensor_tensor(mean[:, :], even, odd, ALU.add).then_inc(s_dv, 1)
                dve.tensor_tensor(std[:, :], stats[:, :, 2], stats[:, :, 5], ALU.add).then_inc(s_dv, 1)
                chain[0] += 2
                link(dve.tensor_tensor(diff[:, :], even, odd, ALU.subtract))
                dve.tensor_scalar(mean[:, :], mean[:, :], 0.5, None, ALU.mult).then_inc(s_dv, 1)
                chain[0] += 1
                link(dve.tensor_tensor(diff[:, :], diff[:, :], diff[:, :], ALU.mult))
                link(dve.scalar_tensor_tensor(std[:, :], diff[:, :], D / 4.0, std[:, :], ALU.mult, ALU.add))
                dve.tensor_scalar(std[:, :], std[:, :], 1.0 / D, EPS, ALU.mult, ALU.add).then_inc(s_ve, 1)
                dve.wait_ge(s_std, k + 1)
                link(dve.reciprocal(rstd[:, :], std[:, :]))
                dve.scalar_tensor_tensor(shift[:, :], mean[:, :], -1.0, rstd[:, :], ALU.mult, ALU.mult).then_inc(s_shift, 1)
                for t in range(TT // 2):
                    dve.tensor_scalar(h[:, t, :], x[:, t, :], mean[:, t:t + 1], rstd[:, t:t + 1],
                                      ALU.subtract, ALU.mult).then_inc(s_h, 1)
                if k in OF_FFN:
                    for b in range(NB):
                        dve.wait_ge(s_hTh, OF_FFN.index(k) * NB + b + 1)
                        cols = slice(b * BK, (b + 1) * BK)
                        dve.tensor_tensor(hTl[:, cols], ps[:, b, :], hTh[:, cols], ALU.subtract).then_inc(s_hT, 1)
                    return
                for b in range(NB // 2):
                    dve.wait_ge(s_tr, NB * k + b + 1)
                    dve.tensor_copy(hT[:, b * BK:(b + 1) * BK], ps[:, b, :]).then_inc(s_hT, 1)

            def ffn(k):
                def mix_experts(c, ft):
                    n = c * FT + (k * NB * FT + ft)
                    dve.wait_ge(s_hid, n + 1)
                    dve.tensor_scalar(r1[:, ft % 2, :], ps[:, HB[ft] + 1, :], 0.0, tv[:, 1:2],
                                      ALU.max, ALU.mult).then_inc(s_r1, 1)
                    dve.wait_ge(s_r1, n + 1)
                    dve.wait_ge(s_r0, n + 1)
                    dve.wait_ge(s_dn, n + 1)
                    dve.scalar_tensor_tensor(r[:, ft, :], r0[:, ft % 2, :], tv[:, 0:1], r1[:, ft % 2, :],
                                             ALU.mult, ALU.add).then_inc(s_r, 1)

                def add_result(c):
                    dve.wait_ge(s_dn, c * FT + (k * NB * FT + 2 * FT))
                    xs = x[:, ds(c * TB, TB), :].rearrange("p a b -> p (a b)")
                    dve.tensor_tensor(xs, ps[:, YB, :], xs, ALU.add).then_inc(s_xf, 1)

                def tokens(c, first=False, last=False):
                    for ft in range(1, FT):
                        mix_experts(c, ft)
                        if k == 0 and not first and ft < 3:
                            dve.wait_ge(s_xf, c + 1)
                            statistics(c - 1, range(2 * ft - 2, 2 * ft))
                    if not last:
                        mix_experts(c + 1, 0)
                    add_result(c)

                mix_experts(0, 0)
                tokens(0, first=True)
                with dve.Fori(1, NB - 1) as c:
                    tokens(c)
                tokens(NB - 1, last=True)
                if k == 0:
                    dve.wait_ge(s_xf, NB + 1)
                    statistics(NB - 1)

            for b in range(NB):
                dve.wait_ge(s_in[b], 16)
                statistics(b)
            ln(0)
            dve.wait_ge(s_wf, 16 * 7)
            link(dve.tensor_copy(idx_f[:, :], idx_i[:, :]))
            link(dve.tensor_scalar(pick[:, :], idx_f[:, :], rowx[:, 0:1], None, ALU.is_equal))
            for e in range(E2):
                dve.tensor_scalar(lbx[:, e, :], lb[:, :], pick[:, e:e + 1], None, ALU.mult).then_inc(s_pick, 1)
            for n, dst in enumerate((cmat, t1)):
                dve.wait_ge(s_ap, n + 1)
                dve.tensor_copy(dst[:, :], ps[:, 4 + n, 0:D]).then_inc(s_az, 1)
            dve.wait_ge(s_ap, 3)
            dve.tensor_scalar(zs[:, :], ps[:, 4, 0:D], float(AD) ** -0.5, None, ALU.mult).then_inc(s_az, 1)
            for e in range(E2):
                dve.wait_ge(s_weffp, e + 1)
                dve.tensor_tensor(weff[:, e, :], ps[:, 6 + e, :], wi[:, :], ALU.add).then_inc(s_weff, 1)
            dve.wait_ge(s_mask, 1)
            link(dve.reduce_max(zrec[:, :], zs[:, :], axis=AX))
            dve.tensor_scalar(zmax[:, :], zrec[:, :], -1.0, None, ALU.mult).then_inc(s_am, 1)
            dve.wait_ge(s_ze, 1)
            dve.wait_ge(s_am, 1)
            link(dve.reciprocal(zrec[:, :], zsum[:, :]))
            dve.tensor_scalar(zn[:, :], ze[:, :], zrec[:, 0:1], None, ALU.mult).then_inc(s_az, 1)
            for n, (dst, bank) in enumerate(((ntm, 5), (mix, 4))):
                dve.wait_ge(s_ap, n + 4)
                dve.tensor_copy(dst[:, :], ps[:, bank, 0:D]).then_inc(s_az, 1)
            for b in range(NB):
                dve.wait_ge(s_mixp, b + 1)
                xs = x[:, b * TB:(b + 1) * TB, :].rearrange("p a b -> p (a b)")
                dve.tensor_tensor(xs, ps[:, b, :], xs, ALU.add).then_inc(s_x1, 1)
                dve.wait_ge(s_x1, b + 1)
                statistics(b)
            dve.sem_inc(s_r, 4)
            ln(1)
            ffn(0)
            ln(2)
            for n in range(2 * HG * NB):
                cols = slice((n % NB) * BK, (n % NB + 1) * BK)
                dve.wait_ge(s_hi, n + 1)
                dve.tensor_tensor(low[:, n // NB, cols], ps[:, n % 4, :], high[:, n // NB, cols],
                                  ALU.subtract).then_inc(s_lo, 1)

            dve.sem_inc(s_maxed, NM)
            dve.sem_inc(s_oT, HG)
            dve.sem_inc(s_orec, 1)

            def maxima(chunk, hd, units=range(U)):
                for u in units:
                    dve.wait_ge(s_sm, chunk * H * U + (hd * U + (u + 1)))
                    dve.reduce_max(mpart[:, ds(hd, 1), u:u + 1], ps[:, MB0 + u % NM, :], axis=AX).then_inc(s_maxed, 1)

            def maxima_and_sum(chunk, hd, q):
                maxima(chunk, hd, range(0, 5))
                sum_of_four(dve, q, 1)
                maxima(chunk, hd, range(5, U))

            def columns(chunk):
                dve.wait_ge(s_maxed, chunk * H * U + (H * U + NM))
                dve.reduce_max(mcol[:, :], mpart[:, :, :].rearrange("p h (t j) -> p (h t) j", t=QT),
                               axis=AX).then_inc(s_mcol, 1)
                dve.wait_ge(s_mcol, chunk + 1)

            def split(chunk):
                dve.wait_ge(s_mT, chunk + 1)
                dve.wait_ge(s_mrow, chunk * MROW)
                mT = ps[0:H * QT, MB0 + 2 % NM, 0:P]
                dve.tensor_scalar(mh[:, :], mT, -1.0, None, ALU.mult).then_inc(s_mneg, 1)
                dve.wait_ge(s_mneg, chunk * 2 + 1)
                dve.scalar_tensor_tensor(ml[:, :], mT, -1.0, mh[:, :], ALU.mult, ALU.subtract).then_inc(s_mneg, 1)

            RP = BK // U

            def reciprocals(chunk, piece):
                dve.wait_ge(s_osum, chunk + 2)
                dve.wait_ge(s_oT, chunk * HG + HG)
                dve.reciprocal(orec[:, ds(piece * RP, RP)], osum[:, ds(piece * RP, RP)]).then_inc(s_orec, 1)

            def normalise(chunk):
                dve.wait_ge(s_oraw, chunk + 2)
                dve.wait_ge(s_orec, chunk * U + (U + 1))
                for g in range(HG):
                    dve.tensor_tensor(oT[:, g, ds(chunk * QC, QC)], oraw[:, g * QC:(g + 1) * QC],
                                      orec[:, g * QC:(g + 1) * QC], ALU.mult).then_inc(s_oT, 1)

            def with_maxima(c, of_last, more=True):
                with dve.Fori(0, KQ - 1) as i:
                    maxima(c + 1, i * 2 + 2)
                    if of_last:
                        reciprocals(c - 1, i * 2)
                    maxima_and_sum(c + 1, i * 2 + 3, c * KQ + i)
                    if of_last:
                        reciprocals(c - 1, i * 2 + 1)
                columns(c + 1)
                if more:
                    maxima(c + 2, 0, range(0, 2))
                split(c + 1)
                if of_last:
                    reciprocals(c - 1, U - 2)
                    reciprocals(c - 1, U - 1)
                if more:
                    maxima(c + 2, 0, range(2, U))
                if of_last:
                    normalise(c - 1)
                if more:
                    maxima_and_sum(c + 2, 1, c * KQ + (KQ - 1))
                else:
                    sum_of_four(dve, c * KQ + (KQ - 1), 1)

            with dve.Fori(0, H) as hd:
                maxima(0, hd)
            columns(0)
            maxima(1, 0, range(0, 2))
            split(0)
            maxima(1, 0, range(2, U))
            maxima(1, 1)
            with_maxima(0, False)
            with dve.Fori(1, NCH - 2) as c:
                with_maxima(c, True)
            with_maxima(NCH - 2, True, more=False)

            def of_second_group(q, four, piece):
                dve.wait_ge(s_quad[1], q + 1)
                sum_of_pair(dve, q, 0, 1)
                reciprocals(NCH - 2, piece)
                dve.wait_ge(s_sum[1], q + 1)
                sum_of_pair(dve, q, 1, 1)
                if four:
                    sum_of_four(dve, q, 1)
                reciprocals(NCH - 2, piece + 1)

            with dve.Fori(0, KQ - 1) as i:
                of_second_group(i + (NCH - 1) * KQ, True, i * 2)
            of_second_group(NCH * KQ - 1, False, U - 2)
            normalise(NCH - 2)
            dve.wait_ge(s_oT, (NCH - 1) * HG + HG)
            for g in range(HG):
                dve.wait_ge(s_sum[g], NCH * KQ + 1)
            for g in range(HG):
                cols = slice(g * QC, (g + 1) * QC)
                link(dve.reciprocal(orec[:, cols], ps[:, SB, cols]))
                dve.wait_ge(s_pv, NCH * KP * 4 + 8)
                dve.tensor_tensor(oT[:, g, (NCH - 1) * QC:], ps[:, OB, cols], orec[:, cols], ALU.mult).then_inc(s_oT, 1)
            for b in range(NB):
                dve.wait_ge(s_wop, b + 1)
                xs = x[:, b * TB:(b + 1) * TB, :].rearrange("p a b -> p (a b)")
                dve.tensor_tensor(xs, ps[:, b, :], xs, ALU.add).then_inc(s_x3, 1)
                dve.wait_ge(s_x3, b + 1)
                statistics(b)
            ln(3)
            ffn(1)

        @block.tensor
        def _(pe):
            mm = pe.matmul

            def transposed(k, then=None):
                for b in range(NB):
                    half = NB // 2
                    if b < half:
                        pe.wait_ge(s_h, TT // 2 * k + (b + 1) * TB)
                    else:
                        pe.wait_ge(s_norm, TT // 2 * k + (b - half + 1) * TB)
                    for t in range(TB):
                        last = pe.transpose(ps[:, b, t * P:(t + 1) * P], h[:, b * TB + t, :], ident[:, :])
                    last.then_inc(s_tr, 1)
                    if then:
                        then(b)

            def ffn(k):
                def hidden(c, ft):
                    pe.wait_ge(s_hT, c + (k * 2 * NB + NB + 1))
                    if ft == 2:
                        pe.wait_ge(s_hT, (k * 2 + 2) * NB)
                    pe.wait_ge(s_r, c * FT + (k * NB * FT + ft + (3 if ft % 2 else 1)))
                    for e in range(E2):
                        for n, (w, h16) in enumerate(((wh, hTh), (wh, hTl), (wl, hTh))):
                            last = mm(ps[:, HB[ft] + e, :], w[:, e, ft * P:(ft + 1) * P],
                                      h16[:, ds(c * BK, BK)], start=(n == 0), stop=(n == 2))
                    last.then_inc(s_hid, 1)

                def down(c, ft):
                    pe.wait_ge(s_r, c * FT + (k * NB * FT + ft + 5))
                    if ft == 0:
                        pe.wait_ge(s_xf, c + (k * NB + 1))
                    for t in range(TB):
                        last = mm(ps[:, YB, t * P:(t + 1) * P], r[:, ft, t * P:(t + 1) * P], wo[:, ft, :],
                                  start=(ft == 0 and t == 0), stop=(ft == FT - 1), skip_group_check=True)
                    last.then_inc(s_dn, 1)

                def chunk(c, more):
                    for ft in range(1, FT):
                        hidden(c, ft)
                        down(c, ft - 1)
                    if more:
                        hidden(c + 1, 0)
                    down(c, FT - 1)

                hidden(0, 0)
                with pe.Fori(0, NB - 1) as c:
                    chunk(c, True)
                chunk(NB - 1, False)

            pe.wait_ge(s_const, 3)

            def lora(e):
                pe.wait_ge(s_pick, e + 1)
                mm(ps[:, 6 + e, :], la[:, :], lbx[:, e, :], start=True, stop=True).then_inc(s_weffp, 1)

            def gram(b):
                for t in range(b * TB, (b + 1) * TB):
                    last = mm(ps[:, 4, 0:D], h[:, t, :], h[:, t, :], start=(t == 0), stop=(t == TT - 1))
                if b == NB - 1:
                    last.then_inc(s_ap, 1)

            transposed(0, gram)
            pe.wait_ge(s_wa, 64)
            pe.wait_ge(s_az, 1)
            mm(ps[:, 5, 0:D], cmat[:, :], awk[:, :], start=True, stop=True).then_inc(s_ap, 1)
            lora(0)
            pe.wait_ge(s_az, 2)
            mm(ps[:, 4, 0:D], t1[:, :], awq[:, :], start=True, stop=True).then_inc(s_ap, 1)
            lora(1)
            pe.wait_ge(s_az, 4)
            mm(ps[:, 5, 0:D], zn[:, :], awv[:, :], start=True, stop=True).then_inc(s_ap, 1)
            pe.wait_ge(s_az, 5)
            mm(ps[:, 4, 0:D], ntm[:, :], awo[:, :], start=True, stop=True).then_inc(s_ap, 1)
            pe.wait_ge(s_az, 6)
            pe.wait_ge(s_hT, NB)
            for b in range(NB):
                for t in range(b * TB, (b + 1) * TB):
                    last = mm(ps[:, b, (t % TB) * P:(t % TB + 1) * P], hT[:, t * P:(t + 1) * P], mix[:, :],
                              start=True, stop=True)
                last.then_inc(s_mixp, 1)
            pe.wait_ge(s_x1, NB)
            pe.sem_inc(s_dn, FT)
            pe.wait_ge(s_wsplit, 1)
            pe.sem_inc(s_xf, 1)
            transposed(1)
            ffn(0)
            pe.wait_ge(s_xf, NB + 1)
            transposed(2)
            pe.wait_ge(s_hT, 3 * NB)
            pe.wait_ge(s_wb, 16 * 5)
            for b in range(NB):
                mm(ps[0:LR, 4 + b, :], bwd[:, :], hT[:, b * BK:(b + 1) * BK], start=True, stop=True).then_inc(s_lat, 1)
            pe.wait_ge(s_latc, NB)
            for n in range(2 * HG * NB):
                slot, b = n // NB, n % NB
                g, of_q = slot // 2, slot % 2
                w, rhs = (bwq, hT) if of_q else (bwk, latT)
                if n >= 4:
                    pe.wait_ge(s_lo, n - 3)
                mm(ps[:, n % 4, :], w[:, g * P:(g + 1) * P], rhs[:, b * BK:(b + 1) * BK],
                   start=True, stop=True).then_inc(s_qk, 1)
            pe.wait_ge(s_lo, 2 * HG * NB)
            pe.sem_inc(s_pv, 8)
            for g in range(HG):
                pe.sem_inc(s_sum[g], 1)
            pe.sem_inc(s_oraw, 1)
            pe.sem_inc(s_osum, 1)

            def score_max(chunk, hd, u):
                t, j = u // 4, u % 4
                pe.wait_ge(s_maxed, chunk * H * U + (hd * U + (u + 1)))
                mm(ps[:, MB0 + u % NM, :], Qs[0:SK, ds(chunk, 1), ds(hd, 1), t * P:(t + 1) * P],
                   Ks[0:SK, ds(hd, 1), j * BK:(j + 1) * BK], start=True, stop=True).then_inc(s_sm, 1)

            def max_transpose(chunk):
                pe.wait_ge(s_mcol, chunk + 1)
                pe.wait_ge(s_maxed, chunk * H * U + (H * U + 3))
                pe.transpose(ps[0:H * QT, MB0 + 2 % NM, 0:P], mcol[:, :], ident[:, :]).then_inc(s_mT, 1)

            def score_exp(chunk, p, u):
                g, k, hp = u // 4, (u // 2) % 2, u % 2
                pe.wait_ge(s_p, (chunk * KP + p) * U + (u + 1))
                for a in range(2):
                    hd = HPG * g + 2 * hp + a
                    last = mm(ps[:, EB0 + u % NE, a * QC:(a + 1) * QC], Ks[0:SR, hd, ds(p * 2 * P + k * P, P)],
                              Qs[0:SR, ds(chunk, 1), hd, :], start=True, stop=True)
                last.then_inc(s_se, 1)

            def weigh(n, odd, g, k):
                if k == 0:
                    pe.wait_ge(s_vst, n * HG + (g + 1))
                pe.wait_ge(s_p, n * U + (NE + 4 * g + 2 * k + 2))
                for j in range(HPG):
                    last = mm(ps[j * HD:(j + 1) * HD, OB, g * QC:(g + 1) * QC], vst[:, g, k, j * HD:(j + 1) * HD],
                              prob[odd][:, k, HPG * g + j, :], start=False, stop=True, skip_group_check=True)
                last.then_inc(s_pv, 1)

            def total(q, g, by_pair=False):
                if by_pair:
                    pe.wait_ge(s_pair[g], q * 2 + 4)
                else:
                    pe.wait_ge(s_quad[g], q + 2)
                for odd in (0, 1) if by_pair else (1,):
                    for j in range(HPG):
                        last = mm(ps[j * HD:(j + 1) * HD, SB, g * QC:(g + 1) * QC], ones[:, :],
                                  pair[:, odd, HPG * g + j, :], start=False, stop=True, skip_group_check=True)
                last.then_inc(s_sum[g], 1)

            def clear(bank):
                mm(ps[:, bank, :], zero16[:, 0:P], zero16[:, :], start=True, stop=True)

            def first(chunk, head_of, rest):
                n, odd = chunk * KP, 0
                pe.wait_ge(s_mrow, chunk * MROW + MROW)
                for u in range(U):
                    if head_of:
                        score_max(*head_of, u)
                    score_exp(chunk, 0, u)
                    if rest and u == 1:
                        weigh(n - 1, 1 - odd, 1, 1)
                    if u == 4:
                        pe.wait_ge(s_oraw, chunk + 1)
                        clear(OB)
                        weigh(n, 0, 0, 0)
                    if u == 6:
                        weigh(n, 0, 0, 1)
                weigh(n, 0, 1, 0)

            SUMS = 0, 2

            ALL, WITH_TRANSPOSE = [[u] for u in range(U)], [[0], [1], [], [], [2], [3], [4, 5], [6, 7]]

            def pair_of_blocks(chunk, p, odd, head_of=None, transpose=False, q=None):
                n = chunk * KP + p
                for u in range(U):
                    if transpose and u == 2:
                        max_transpose(chunk + 1)
                    if transpose and u == 4:
                        pe.wait_ge(s_mneg, chunk * 2 + 4)
                    if head_of:
                        for v in (WITH_TRANSPOSE if transpose else ALL)[u]:
                            score_max(*head_of, v)
                    score_exp(chunk, p, u)
                    if u == 1:
                        weigh(n - 1, 1 - odd, 1, 1)
                    if u == 3:
                        weigh(n, odd, 0, 0)
                    if u == 5:
                        weigh(n, odd, 0, 1)
                    if u == 7:
                        weigh(n, odd, 1, 0)
                    for g in range(HG):
                        if q is not None and u == SUMS[g]:
                            total(q, g)

            def rest_of_chunk(chunk, of_last, more, next_is_last=False):
                def head(p):
                    return (chunk + 1, p + 1) if more else None

                pair_of_blocks(chunk, 1, 1, head(1), q=chunk * KQ - 1 if of_last else None)
                pair_of_blocks(chunk, 2, 0, head(2))
                pe.wait_ge(s_osum, chunk + 1)
                clear(SB)
                with pe.Fori(1, KQ - 1) as i:
                    pair_of_blocks(chunk, i * 2 + 1, 1, head(i * 2 + 1), q=chunk * KQ + i - 1)
                    pair_of_blocks(chunk, i * 2 + 2, 0, head(i * 2 + 2))
                pair_of_blocks(chunk, KP - 1, 1, (chunk + 2, 0) if more and not next_is_last else None, more,
                               q=chunk * KQ + (KQ - 2))

            def values(n, k):
                if k == 0:
                    pe.wait_ge(s_lst, n + 1)
                    pe.wait_ge(s_vc, n + 1)
                last = mm(ps[:, VB, k * H * HD:(k + 1) * H * HD], lst[:, k * P:(k + 1) * P], bwv[:, :],
                          start=True, stop=True)
                if k:
                    last.then_inc(s_vp, 1)

            pe.sem_inc(s_vc, 1)
            pe.sem_inc(s_vp, 1)
            for g in range(HG):
                pe.wait_ge(s_stack[g], 16 * 4 * HPG)
                pe.wait_ge(s_lows[g], 16 * 2 * HPG)
                with pe.Fori(g * HPG, (g + 1) * HPG) as hd:
                    for u in range(U):
                        score_max(0, hd, u)
                        if u == 2 or u == 6:
                            values(hd, u // 4)
            pe.wait_ge(s_vc, KP + 1)
            for u in range(U):
                if u == 2:
                    max_transpose(0)
                    pe.wait_ge(s_mneg, 2)
                score_max(1, 0, u)
            first(0, (1, 1), False)
            rest_of_chunk(0, False, True)
            with pe.Fori(1, NCH - 2) as c:
                first(c, (c + 1, 1), True)
                rest_of_chunk(c, True, True)
            first(NCH - 2, (NCH - 1, 1), True)
            rest_of_chunk(NCH - 2, True, True, next_is_last=True)
            first(NCH - 1, None, True)
            rest_of_chunk(NCH - 1, True, False)
            weigh(NCH * KP - 1, 1, 1, 1)
            for g in range(HG):
                total(NCH * KQ - 1, g, by_pair=True)

            pe.wait_ge(s_maxed, NCH * H * U + NM)
            for b in range(NB):
                pe.wait_ge(s_oT, HG * ((b + 1) * BK // QC + 1))
                for t in range(b * TB, (b + 1) * TB):
                    for g in range(HG):
                        last = mm(ps[:, b, (t % TB) * P:(t % TB + 1) * P], oT[:, g, t * P:(t + 1) * P], bwo[:, g, :],
                                  start=(g == 0), stop=(g == HG - 1))
                last.then_inc(s_wop, 1)
            transposed(3)
            ffn(1)


def kernel(**inputs):
    import concourse.bacc as bacc
    from concourse.bass_utils import run_bass_kernel_spmd

    a = {k: np.asarray(v) for k, v in inputs.items()}
    T = lambda v: np.ascontiguousarray(v.T)
    x = a["L0_attn_a_x"]
    experts, rank, d = a["L0_ffn_lora_As"].shape
    f = a["L0_ffn_lora_Bs"].shape[1]
    arrays = {
        "x_in": np.ascontiguousarray(x.reshape(-1, d)),
        "a_wqT": T(a["L0_attn_a_Wq"]), "a_wkT": T(a["L0_attn_a_Wk"]),
        "a_wv": np.ascontiguousarray(a["L0_attn_a_Wv"]), "a_woT": T(a["L0_attn_a_Wo"]),
        "b_wqT": T(a["L0_attn_b_Wq"]), "b_wdT": T(a["L0_attn_b_Wkv_down"]),
        "b_wkT": T(a["L0_attn_b_Wk_up"]), "b_wvT": T(a["L0_attn_b_Wv_up"]), "b_woT": T(a["L0_attn_b_Wo"]),
        "wiT": T(a["L0_ffn_wi_w"]), "woT": T(a["L0_ffn_wo_w"]),
        "lora_a": np.ascontiguousarray(a["L0_ffn_lora_As"].reshape(experts * rank, d)),
        "lora_bT": np.ascontiguousarray(a["L0_ffn_lora_Bs"].transpose(0, 2, 1).reshape(experts * rank, f)),
        "top_idx": np.ascontiguousarray(a["L0_ffn_top_k_indices"]),
        "top_val": np.ascontiguousarray(a["L0_ffn_top_k_values"]),
        "row_expert": np.repeat(np.arange(experts, dtype=np.float32), rank)[:, None],
    }
    nc = bacc.Bacc("TRN2", target_bir_lowering=False, num_devices=1)
    aps = [nc.dram_tensor(k, v.shape, mybir.dt.from_np(v.dtype), kind="ExternalInput").ap() for k, v in arrays.items()]
    out = nc.dram_tensor("out", arrays["x_in"].shape, mybir.dt.float32, kind="ExternalOutput").ap()
    build(nc, *aps, out)
    r = run_bass_kernel_spmd(nc, [arrays], core_ids=[0])
    return r.results[0]["out"].reshape(x.shape)
```
